# Optimizing a Trainium2 kernel written in Bass

```python
import numpy as np
import jax
import jax.numpy as jnp

def _softmax(x, axis=-1):
    return jax.nn.softmax(x, axis=axis)

def _gelu(x):
    return jax.nn.gelu(x, approximate=True)

def _silu(x):
    return jax.nn.silu(x)

def _sigmoid(x):
    return jax.nn.sigmoid(x)

def _layernorm(x, axis=-1, eps=1e-05):
    m = jnp.mean(x, axis=axis, keepdims=True)
    v = jnp.var(x, axis=axis, keepdims=True)
    return (x - m) / jnp.sqrt(v + eps)

def _scatter_add(tgt, idx, src, axis=0):
    return tgt.at[idx].add(src)

def _segment_sum(src, seg, n):
    return jax.ops.segment_sum(src, seg, n)
kernel_name = 'mk_macaron_d1_jaxref_r8_138754'

def setup_inputs(seed: int=0):
    np.random.seed(seed)
    _w = jnp.asarray

    def _L0_attn_setup():
        import jax, jax.numpy as jnp
        import numpy as np
        N_EMBD = 128
        N_HEAD = 16
        LATENT = 64
        HEAD_DIM = N_EMBD // N_HEAD
        B, T = (2, 256)
        SCALE = 1.0 / np.sqrt(LATENT)
        key = jax.random.key(seed)
        ks = jax.random.split(key, 10)
        s = lambda fan_in: 1.0 / np.sqrt(fan_in)
        return {'x': jax.random.normal(ks[0], (B, T, N_EMBD), dtype=jnp.float32), 'Wq': jax.random.normal(ks[1], (N_EMBD, N_EMBD), dtype=jnp.float32) * s(N_EMBD), 'bq': jnp.zeros((N_EMBD,), dtype=jnp.float32), 'Wk': jax.random.normal(ks[2], (N_EMBD, N_HEAD * LATENT), dtype=jnp.float32) * s(N_EMBD), 'bk': jnp.zeros((N_HEAD * LATENT,), dtype=jnp.float32), 'Wv': jax.random.normal(ks[3], (N_EMBD, N_HEAD * LATENT), dtype=jnp.float32) * s(N_EMBD), 'bv': jnp.zeros((N_HEAD * LATENT,), dtype=jnp.float32), 'Wo': jax.random.normal(ks[4], (N_HEAD * LATENT, N_EMBD), dtype=jnp.float32) * s(N_HEAD * LATENT), 'bo': jnp.zeros((N_EMBD,), dtype=jnp.float32), 'Wc': jax.random.normal(ks[5], (HEAD_DIM, LATENT), dtype=jnp.float32) * s(HEAD_DIM)}
    _L0_attn_in = _L0_attn_setup()

    def _L0_ffn_setup():
        import jax, jax.numpy as jnp
        import numpy as np
        B, S, D = (2, 256, 128)
        E, G, K = (32, 8, 4)
        H, SH = (256, 256)
        CAP_FACTOR = 1.25

        def _l2norm(v):
            n = jnp.linalg.norm(v, axis=-1, keepdims=True)
            return v / jnp.maximum(n, 1e-12)
        key = jax.random.key(seed)
        ks = jax.random.split(key, 10)
        x = jax.random.normal(ks[0], (B, S, D), jnp.float32)
        group_centroids = jax.random.normal(ks[1], (G, D), jnp.float32) * 0.02
        expert_centroids = jax.random.normal(ks[2], (E, D), jnp.float32) * 0.02
        bias = jnp.zeros((E,), jnp.float32)
        sd_in = 1.0 / np.sqrt(D).astype(np.float32)
        sd_h = 1.0 / np.sqrt(H).astype(np.float32)
        wg = jax.random.normal(ks[3], (E, D, H), jnp.float32) * sd_in
        wu = jax.random.normal(ks[4], (E, D, H), jnp.float32) * sd_in
        wd = jax.random.normal(ks[5], (E, H, D), jnp.float32) * sd_h
        sg = jax.random.normal(ks[6], (D, SH), jnp.float32) * sd_in
        su = jax.random.normal(ks[7], (D, SH), jnp.float32) * sd_in
        sd_w = jax.random.normal(ks[8], (SH, D), jnp.float32) * sd_h
        return dict(x=x, group_centroids=group_centroids, expert_centroids=expert_centroids, bias=bias, wg=wg, wu=wu, wd=wd, sg=sg, su=su, sd=sd_w)
    _L0_ffn_in = _L0_ffn_setup()
    _d = {'L0_attn_x': _L0_attn_in['x'], 'L0_attn_Wq': _L0_attn_in['Wq'], 'L0_attn_bq': _L0_attn_in['bq'], 'L0_attn_Wk': _L0_attn_in['Wk'], 'L0_attn_bk': _L0_attn_in['bk'], 'L0_attn_Wv': _L0_attn_in['Wv'], 'L0_attn_bv': _L0_attn_in['bv'], 'L0_attn_Wo': _L0_attn_in['Wo'], 'L0_attn_bo': _L0_attn_in['bo'], 'L0_attn_Wc': _L0_attn_in['Wc'], 'L0_ffn_group_centroids': _L0_ffn_in['group_centroids'], 'L0_ffn_expert_centroids': _L0_ffn_in['expert_centroids'], 'L0_ffn_bias': _L0_ffn_in['bias'], 'L0_ffn_wg': _L0_ffn_in['wg'], 'L0_ffn_wu': _L0_ffn_in['wu'], 'L0_ffn_wd': _L0_ffn_in['wd'], 'L0_ffn_sg': _L0_ffn_in['sg'], 'L0_ffn_su': _L0_ffn_in['su'], 'L0_ffn_sd': _L0_ffn_in['sd']}
    _x0 = _d['L0_attn_x']
    _d['L0_attn_x'] = jax.random.normal(jax.random.fold_in(jax.random.key(seed), 1), (2, 1024, 128), dtype=_x0.dtype)
    del _x0
    return _d

def reference(L0_attn_x, L0_attn_Wq, L0_attn_bq, L0_attn_Wk, L0_attn_bk, L0_attn_Wv, L0_attn_bv, L0_attn_Wo, L0_attn_bo, L0_attn_Wc, L0_ffn_group_centroids, L0_ffn_expert_centroids, L0_ffn_bias, L0_ffn_wg, L0_ffn_wu, L0_ffn_wd, L0_ffn_sg, L0_ffn_su, L0_ffn_sd):

    def _L0_attn_ref(x, Wq, bq, Wk, bk, Wv, bv, Wo, bo, Wc):
        import jax, jax.numpy as jnp
        import numpy as np
        N_EMBD = 128
        N_HEAD = 16
        LATENT = 64
        HEAD_DIM = N_EMBD // N_HEAD
        B, T = (2, 256)
        SCALE = 1.0 / np.sqrt(LATENT)
        Bv, Tv, C = x.shape
        q = (x @ Wq + bq).reshape(Bv, Tv, N_HEAD, HEAD_DIM)
        k = (x @ Wk + bk).reshape(Bv, Tv, N_HEAD, LATENT)
        v = (x @ Wv + bv).reshape(Bv, Tv, N_HEAD, LATENT)
        qc = jnp.einsum('bthd,dl->bthl', q, Wc)
        att = jnp.einsum('bthl,bshl->bhts', qc, k) * SCALE
        causal = jnp.tril(jnp.ones((Tv, Tv), dtype=bool))
        att = jnp.where(causal[None, None], att, -jnp.inf)
        att = jax.nn.softmax(att, axis=-1)
        y = jnp.einsum('bhts,bshl->bthl', att, v).reshape(Bv, Tv, N_HEAD * LATENT)
        return y @ Wo + bo

    def _L0_ffn_ref(x, group_centroids, expert_centroids, bias, wg, wu, wd, sg, su, sd):
        import jax, jax.numpy as jnp
        import numpy as np
        B, S, D = (2, 256, 128)
        E, G, K = (32, 8, 4)
        H, SH = (256, 256)
        CAP_FACTOR = 1.25

        def _l2norm(v):
            n = jnp.linalg.norm(v, axis=-1, keepdims=True)
            return v / jnp.maximum(n, 1e-12)
        b, s, d = x.shape
        xf = x.reshape(-1, d)
        N = xf.shape[0]
        shared = jax.nn.silu(xf @ sg) * (xf @ su) @ sd
        xn = _l2norm(xf)
        group_scores = xn @ _l2norm(group_centroids).T
        n_top_groups = max(1, G // 2)
        _, top_group_idx = jax.lax.top_k(group_scores, n_top_groups)
        expert_scores = xn @ _l2norm(expert_centroids).T + bias
        expert_to_group = jnp.arange(E) // (E // G)
        sel = jnp.zeros((N, G), xf.dtype).at[jnp.arange(N)[:, None], top_group_idx].set(1.0)
        group_mask = sel[:, expert_to_group]
        masked = expert_scores * group_mask + (1.0 - group_mask) * -1000000000.0
        top_scores, top_idx = jax.lax.top_k(masked, K)
        gates = jax.nn.softmax(top_scores, axis=-1)
        capacity = max(1, int(N / E * K * CAP_FACTOR))
        flat_e = top_idx.reshape(-1)
        flat_g = gates.reshape(-1)
        tok = jnp.repeat(jnp.arange(N), K)
        onehot = jax.nn.one_hot(flat_e, E, dtype=jnp.int32)
        pos = jnp.cumsum(onehot, axis=0)[jnp.arange(N * K), flat_e] - 1
        keep = pos < capacity
        e_s = jnp.where(keep, flat_e, E)
        p_s = jnp.where(keep, pos, 0)
        buf = jnp.zeros((E + 1, capacity, d), xf.dtype).at[e_s, p_s].set(xf[tok])[:E]
        h = jax.nn.silu(jnp.einsum('ecd,edh->ech', buf, wg)) * jnp.einsum('ecd,edh->ech', buf, wu)
        out_e = jnp.einsum('ech,ehd->ecd', h, wd)
        gathered = out_e[flat_e, jnp.minimum(pos, capacity - 1)]
        contrib = gathered * (flat_g * keep.astype(xf.dtype))[:, None]
        routed = jnp.zeros_like(xf).at[tok].add(contrib)
        return (shared + routed).reshape(b, s, d)
    x = L0_attn_x
    x = x + 0.5 * _L0_ffn_ref(_layernorm(x, axis=-1), L0_ffn_group_centroids, L0_ffn_expert_centroids, L0_ffn_bias, L0_ffn_wg, L0_ffn_wu, L0_ffn_wd, L0_ffn_sg, L0_ffn_su, L0_ffn_sd)
    x = x + _L0_attn_ref(_layernorm(x, axis=-1), L0_attn_Wq, L0_attn_bq, L0_attn_Wk, L0_attn_bk, L0_attn_Wv, L0_attn_bv, L0_attn_Wo, L0_attn_bo, L0_attn_Wc)
    x = x + 0.5 * _L0_ffn_ref(_layernorm(x, axis=-1), L0_ffn_group_centroids, L0_ffn_expert_centroids, L0_ffn_bias, L0_ffn_wg, L0_ffn_wu, L0_ffn_wd, L0_ffn_sg, L0_ffn_su, L0_ffn_sd)
    return x

_drawn_inputs = setup_inputs


def setup_inputs(seed=0):
    import zlib

    import numpy as np

    out = dict(_drawn_inputs(seed))
    spreads = {'L0_attn_bq': (0.0, 0.367),
     'L0_attn_bk': (0.0, 0.8),
     'L0_attn_bv': (0.0, 0.1),
     'L0_attn_bo': (0.0, 0.1),
     'L0_ffn_bias': (0.0, 0.1)}
    factors = {}
    for name, (base, spread) in spreads.items():
        noise = np.random.default_rng([zlib.crc32(name.encode()), seed]).standard_normal(out[name].shape)
        drawn = base * np.exp(spread * noise) if base else spread * noise
        out[name] = jnp.asarray(drawn.astype(out[name].dtype))
    for name, factor in factors.items():
        out[name] = (out[name] * factor).astype(out[name].dtype)
    return out
```

```python
from contextlib import ExitStack

import concourse.bass as bass
from concourse import mybir

F32 = mybir.dt.float32
F32R = mybir.dt.float32r
BF16 = mybir.dt.bfloat16
U32 = mybir.dt.uint32
I32 = mybir.dt.int32
ALU = mybir.AluOpType
ACT = mybir.ActivationFunctionType
AX = mybir.AxisListType

P = 128
B, T, D = 2, 1024, 128
NT = B * T // P
HT = T // P
E, G, K = 32, 8, 4
EG = E // G
KG = G // 2
HID = 256
HC = HID // P
CAP = int(B * T / E * K * 1.25)
PAIR = 2 * CAP
PT = PAIR // P
NPAIR = E // 2
SLOTS = E * CAP
SKIP = 2 * SLOTS
NH, LAT, HD = 16, 64, 8
HG = 4
NG = NH // HG
RW = 32
R0 = 2
VW = LAT + 1
SCALE = 1.0 / 8.0
NEG = -1.0e30

C_ID, C_TRI, C_CS, C_CT, C_I8, C_I32 = 0, 128, 256, 384, 512, 520
C_SQ, C_LQ, C_SK, C_LK, C_S2, C_L2, C_EPS, C_ONE, C_N = 552, 553, 554, 555, 556, 557, 558, 560, 688

ROWS = [(i, c, min(512, (i + 1) * P) if c == 0 else (i - 3) * P) for i in range(HT) for c in range(1 + i // 4)]
NS = 2 * len(ROWS)
CHUNKS = [(j, j * P, 512 - j * P, 0) for j in range(4)] + \
         [(j, max(512, j * P), 1024 - max(512, j * P), 1) for j in range(8)]
NC = len(CHUNKS)
SLOT = HG * NC


def s_steps_at(n):
    return range(3 * (n - 4) // 4, 3 * (n - 3) // 4) if 4 <= n < 36 else range(0)


def program(nc, x, Wq, bq, WkT, bk, Wv, bv, Wo, bo, WcT, gcen, ecen, ebias, wg, wu, wd, sg, su, sd, consts, out):
    xbuf = nc.dram_tensor("xbuf", [SLOTS, D], F32).ap()
    ybuf = nc.dram_tensor("ybuf", [SLOTS, D], F32).ap()
    x_t = x.rearrange("b (n p) d -> p (b n) d", p=P)
    out_t = out.rearrange("b (n p) d -> p (b n) d", p=P)

    with ExitStack() as ctx:
        def sb(name, shape, dt=F32):
            return ctx.enter_context(nc.sbuf_tensor(name, shape, dt))

        def sem(name):
            return ctx.enter_context(nc.semaphore(name))

        PS = ctx.enter_context(nc.psum_tensor("PS", [P, 8, 512], F32))

        def flat(b0, n):
            return PS[:, b0:b0 + n, :].rearrange("p b n -> p (b n)")

        cst = sb("cst", [P, C_N])
        identb = sb("identb", [P, P], BF16)
        trib = sb("trib", [P, P], BF16)
        onesb = sb("onesb", [P, P], BF16)
        causS = sb("causS", [P, P], BF16)
        causT = sb("causT", [P, P], BF16)
        xs = sb("xs", [P, NT, D])
        xn = sb("xn", [P, NT, D])
        xnT = sb("xnT", [P, NT * P])
        cen = sb("cen", [G + E, D])
        cenn = sb("cenn", [G + E, D])
        cenT = sb("cenT", [P, G + E])
        csq = sb("csq", [G + E, 4])
        ebb = sb("ebb", [P, E])
        st = sb("st", [P, HT, 6])
        mv = sb("mv", [P, HT, 2])
        std = sb("std", [P, HT])
        rstd = sb("rstd", [P, HT])
        sqj = sb("sqj", [P, D])
        ssq = sb("ssq", [P, HT])
        nrm = sb("nrm", [P, 2, HT])
        rn = sb("rn", [P, HT])
        gs = sb("gs", [P, HT, G])
        es = sb("es", [P, HT, E])
        v8 = sb("v8", [P, HT, 8])
        i8 = sb("i8", [P, HT, 8], U32)
        idf = sb("idf", [P, HT, K])
        eif = sb("eif", [P, HT, K])
        gm = sb("gm", [P, HT, G])
        pen = sb("pen", [P, HT, G])
        mk = sb("mk", [P, HT, E])
        sel = sb("sel", [P, NT, E], BF16)
        gd = sb("gd", [P, 2, HT, K])
        ge = sb("ge", [P, 2, HT, K])
        gsum = sb("gsum", [P, HT])
        pos = sb("pos", [P, HT * K])
        over = sb("over", [P, HT * K])
        keep = sb("keep", [P, HT * K])
        slf = sb("slf", [P, HT * K])
        gate = sb("gate", [P, 2, HT * K])
        sidx = sb("sidx", [P, 2, HT * K], I32)
        gidx = sb("gidx", [P, 2, HT * K], I32)
        sgw = sb("sgw", [P, HID])
        suw = sb("suw", [P, HID])
        sdw = sb("sdw", [P, HC, D])
        yg = sb("yg", [P, HT, K, D])
        wq_in = sb("wq_in", [P, NH, HD])
        wv_in = sb("wv_in", [P, NH * LAT])
        wo_in = sb("wo_in", [P, 8, D])
        wcT = sb("wcT", [P, 2, HD])
        bk2 = sb("bk2", [P, 8, 2])
        bvc = sb("bvc", [P, 8])
        bor = sb("bor", [1, D])
        brow = sb("brow", [1, D])
        bq2 = sb("bq2", [2, NH, HD])
        wqx = sb("wqx", [P, NH, RW])
        wkx = sb("wkx", [P, NH, RW])
        bqf = sb("bqf", [2, NH, RW])
        bkf = sb("bkf", [2, NH, RW])
        bqs = sb("bqs", [2, NH * RW])
        bqx = sb("bqx", [2, NH * RW], F32R)
        bkx = sb("bkx", [2, NH * RW], F32R)
        ones2 = sb("ones2", [2, 512], F32R)
        Qn = sb("Qn", [P, T], F32R)
        Kn = sb("Kn", [P, T], F32R)
        Qc = [sb(f"Qc{i}", [P, T], F32R) for i in range(2)]
        Kz = [sb(f"Kz{i}", [P, HG, T], F32R) for i in range(2)]
        mxp = sb("mxp", [P, HT, 2, HG])
        mxm = sb("mxm", [P, HT, HG])
        M = sb("M", [P, HT, HG, RW])
        pT = sb("pT", [P, 4, 512])
        rec = sb("rec", [P, 2, 4, 1])
        area_o = sb("area_o", [P, HT * NH * LAT])
        area_v = sb("area_v", [P, HT * NH * VW + P - VW])

        def parts(area, first, *shapes):
            views, at = [], first
            for shape, pattern, sizes in shapes:
                v = area[:, at:at + shape]
                views.append(v.rearrange(pattern, **sizes) if pattern else v)
                at += shape
            assert at <= area.shape[1]
            return views

        os_ = area_o[:].rearrange("p (i n) -> p i n", i=HT)
        vs = area_v[:, 0:HT * NH * VW].rearrange("p (j h l) -> p j h l", j=HT, h=NH)
        half = ("p (c n) -> p c n", dict(c=HC))
        sil0, sil1, hb0, hb1 = parts(area_o, 0, *[(HC * 512, *half)] * 4)
        sil, hb = [sil0, sil1], [hb0, hb1]
        xeT0, xeT1 = parts(area_o, 4 * HC * 512, *[(PAIR, None, None)] * 2)
        xeT = [xeT0, xeT1]
        rows = (PAIR, "p (t d) -> p t d", dict(d=D))
        yo0, yo1, oh = parts(area_o, 4 * HC * 512 + 2 * PAIR, rows, rows, (HT * K * E, "p (n e) -> p n e", dict(e=E)))
        yo = [yo0, yo1]
        wkT, = parts(area_o, 0, (NH * LAT, None, None))
        wide = (2 * HID, "p (a n) -> p a n", dict(a=2))
        deep = (2 * HC * D, "p (a c n) -> p a c n", dict(a=2, c=HC))
        wgt0, wgt1, wut0, wut1, wdt0, wdt1, xe0, xe1, pc, geq = parts(
            area_v, 0, wide, wide, wide, wide, deep, deep, rows, rows,
            (HT * K * E, "p (n e) -> p n e", dict(e=E)), (HT * K * G, "p (n e) -> p n e", dict(e=G)))
        wgt, wut, wdt, xe = [wgt0, wgt1], [wut0, wut1], [wdt0, wdt1], [xe0, xe1]
        yT = parts(area_v, 0, (T, None, None), (T, None, None))

        s_const = sem("s_const")
        s_x = sem("s_x")
        s_cen = sem("s_cen")
        s_w = sem("s_w")
        s_zero = sem("s_zero")
        s_fill = sem("s_fill")
        s_cst = sem("s_cst")
        s_dve = sem("s_dve")
        s_act = sem("s_act")
        s_cn = sem("s_cn")
        s_cnn = sem("s_cnn")
        s_ct = sem("s_ct")
        s_ctc = sem("s_ctc")
        s_wk = sem("s_wk")
        s_ax = sem("s_ax")
        ln_stat = sem("ln_stat")
        ln_std = sem("ln_std")
        xn_ready = sem("xn_ready")
        xnT_ps = sem("xnT_ps")
        xnT_ready = sem("xnT_ready")
        nrm_ready = sem("nrm_ready")
        sc_ready = sem("sc_ready")
        sel_ready = sem("sel_ready")
        gd_ready = sem("gd_ready")
        ge_ready = sem("ge_ready")
        cum_ready = sem("cum_ready")
        slot_ready = sem("slot_ready")
        scat = sem("scat")
        sh_gu = sem("sh_gu")
        sh_sil = sem("sh_sil")
        sh_h = sem("sh_h")
        sh_y = sem("sh_y")
        sh_x = sem("sh_x")
        w_in = [sem(f"w_in{j}") for j in range(2)]
        x_in = [sem(f"x_in{j}") for j in range(2)]
        in_free = sem("in_free")
        xeT_ps = sem("xeT_ps")
        xeT_sb = sem("xeT_sb")
        gu_ready = sem("gu_ready")
        sil_ready = sem("sil_ready")
        h_ready = sem("h_ready")
        y_ps = sem("y_ps")
        y_sb = sem("y_sb")
        y_out = [sem(f"y_out{j}") for j in range(2)]
        gath = [sem(f"gath{t}") for t in range(HT)]
        comb = sem("comb")
        v_ps = sem("v_ps")
        v_a = sem("v_a")
        v_d = sem("v_d")
        qk_ps = sem("qk_ps")
        tq_ready = sem("tq_ready")
        qk_split = sem("qk_split")
        kz_ready = sem("kz_ready")
        s_ready = sem("s_ready")
        smax = sem("smax")
        m_ready = sem("m_ready")
        mt_ready = sem("mt_ready")
        qc_ready = sem("qc_ready")
        st_ready = sem("st_ready")
        exp_done = sem("exp_done")
        pv_done = sem("pv_done")
        norm_done = sem("norm_done")
        yt_ps = sem("yt_ps")
        yt_a = sem("yt_a")
        yt_d = sem("yt_d")
        wo_ps = sem("wo_ps")
        wo_x = sem("wo_x")
        s_out = sem("s_out")

        ident = cst[:, C_ID:C_ID + P]
        block = ctx.enter_context(nc.Block())
        N_W = 13 * 16

        @block.sync
        def _(sp):
            sp.dma_start(cst[:], consts).then_inc(s_const, 16)
            for h in range(4):
                sp.dma_start(xs[:, 4 * h:4 * h + 4, :], x_t[:, 4 * h:4 * h + 4, :]).then_inc(s_x, 16)
            sp.dma_start(cen[0:G, :], gcen).then_inc(s_cen, 16)
            sp.dma_start(cen[G:G + E, :], ecen).then_inc(s_cen, 16)
            sp.dma_start(ebb[:], ebias.partition_broadcast(P)).then_inc(s_cen, 16)
            sp.wait_ge(s_zero, 3)
            zt = Kz[0][:].rearrange("p h t -> p (h t)").bitcast(F32)
            zrow = SLOTS * D // P
            xb_flat = xbuf.rearrange("(p c) d -> p (c d)", p=P)
            for k in range(0, zrow, 2560):
                sp.dma_start(xb_flat[:, k:k + 2560], zt[:, 0:2560]).then_inc(s_fill, 16)
            sp.dma_start(sgw[:], sg).then_inc(s_w, 16)
            sp.dma_start(suw[:], su).then_inc(s_w, 16)
            sp.dma_start(sdw[:], sd.rearrange("(c p) d -> p c d", p=P)).then_inc(s_w, 16)
            sp.dma_start(wkT, WkT).then_inc(s_w, 16)
            sp.dma_start(wq_in[:].rearrange("p h d -> p (h d)"), Wq).then_inc(s_w, 16)
            sp.dma_start(wv_in[:], Wv).then_inc(s_w, 16)
            sp.dma_start(wo_in[:], Wo.rearrange("(c p) d -> p c d", p=P)).then_inc(s_w, 16)
            for a in range(2):
                sp.dma_start(wcT[a * LAT:(a + 1) * LAT, a, :], WcT).then_inc(s_w, 16)
            sp.dma_start(bq2[:].rearrange("a h d -> a (h d)"), bq).then_inc(s_w, 16)
            sp.dma_start(bk2[:], bk).then_inc(s_w, 16)
            sp.dma_start(bvc[:], bv).then_inc(s_w, 16)
            sp.dma_start(bor[:], bo.rearrange("(a n) -> a n", a=1)).then_inc(s_w, 16)

            def pair_in(L, n, j):
                sp.wait_ge(in_free, n + (NPAIR * L + 1))
                sp.dma_start(wgt[j], wg[bass.ds(n * 2, 2)].rearrange("e p h -> p e h")).then_inc(w_in[j], 16)
                sp.dma_start(wut[j], wu[bass.ds(n * 2, 2)].rearrange("e p h -> p e h")).then_inc(w_in[j], 16)
                for a in range(2):
                    sp.dma_start(wdt[j][:, a], wd[bass.ds(n * 2 + a, 1)].rearrange("e (c p) d -> p (e c) d", p=P))\
                        .then_inc(w_in[j], 16)
                sp.wait_ge(scat, 64 * 16 * (L + 1))
                sp.dma_start(xe[j], xbuf[bass.ds(n * PAIR, PAIR)].rearrange("(c p) d -> p c d", p=P)).then_inc(x_in[j], 16)

            def pair_out(L, n, j):
                sp.wait_ge(y_sb, n * 2 + (2 * NPAIR * L + 4))
                sp.dma_start(ybuf[bass.ds(n * PAIR, PAIR)].rearrange("(c p) d -> p c d", p=P), yo[j]).then_inc(y_out[j], 16)

            def expert_pairs(L):
                for j in range(2):
                    pair_in(L, j, j)
                with sp.Fori(0, NPAIR // 2 - 1) as it:
                    for j in range(2):
                        pair_out(L, it * 2 + j, j)
                        pair_in(L, it * 2 + (j + 2), j)
                for j in range(2):
                    pair_out(L, NPAIR - 2 + j, j)

            expert_pairs(0)
            for Gi in range(B * NG):
                sp.wait_ge(qk_split, 2 * Gi + 2)
                sp.wait_ge(s_fill, 64)
                for h in range(HG):
                    sp.dma_start(Kz[Gi % 2][RW * h:RW * h + RW, h, :].bitcast(F32),
                                 Kn[RW * h:RW * h + RW, :].bitcast(F32)).then_inc(kz_ready, 16)
            sp.wait_ge(wo_x, 2 * HT)
            expert_pairs(1)
            for t in range(NT):
                sp.wait_ge(comb, NT + t + 1)
                sp.dma_start(out_t[:, t, :], xs[:, t, :]).then_inc(s_out, 16)
            sp.wait_ge(s_out, 16 * NT)

        @block.gpsimd
        def _(pool):
            for k in range(2):
                nc.gpsimd.memset(Kz[k][:].rearrange("p h t -> p (h t)").bitcast(F32), 0.0).then_inc(s_zero, 1)

            def scatter(L, H, lo, hi):
                pool.wait_ge(slot_ready, 2 * L + H + 1)
                pool.wait_ge(s_fill, 16 * 4)
                for t in range(lo, hi):
                    for k in range(K):
                        pool.indirect_dma_start(
                            xbuf[:, :], bass.IndirectOffsetOnAxis(ap=sidx[:, H, t * K + k:t * K + k + 1], axis=0),
                            xn[:, H * HT + t, :], None, bounds_check=SLOTS - 1, oob_is_err=False).then_inc(scat, 16)

            def gather(L, H, lo, hi):
                if lo == 0:
                    for j in range(2):
                        pool.wait_ge(y_out[j], 16 * NPAIR // 2 * (L + 1) + 16)
                for t in range(lo, hi):
                    if 2 * L + H > 0:
                        pool.wait_ge(comb, (2 * L + H - 1) * HT + t + 1)
                    for k in range(K):
                        pool.indirect_dma_start(
                            yg[:, t, k, :], None, ybuf[:, :],
                            bass.IndirectOffsetOnAxis(ap=gidx[:, H, t * K + k:t * K + k + 1], axis=0),
                            bounds_check=SLOTS - 1, oob_is_err=False).then_inc(gath[t], 16)

            scatter(0, 0, 0, HT)
            scatter(0, 1, 0, HT)
            gather(0, 0, 0, HT)
            gather(0, 1, 0, HT)
            scatter(1, 0, 0, HT)
            scatter(1, 1, 0, HT)
            gather(1, 0, 0, HT)
            gather(1, 1, 0, HT)

        @block.scalar
        def _(act):
            act.wait_ge(s_const, 16)
            act.wait_ge(s_cen, 48)
            nc.scalar.activation(cenn[:], cen[:], ACT.Square, accum_out=csq[:, 0:1]).then_inc(s_act, 1)
            act.wait_ge(s_act, 1)
            nc.scalar.activation(csq[:, 1:2], csq[:, 0:1], ACT.Sqrt).then_inc(s_cn, 1)

            def ln(r, H, norms):
                act.wait_ge(ln_stat, r + 1)
                nc.scalar.activation(std[:], mv[:, :, 1], ACT.Sqrt, bias=cst[:, C_EPS:C_EPS + 1]).then_inc(ln_std, 1)
                for q in range(2):
                    act.wait_ge(xnT_ps, 2 * r + q + 1)
                    nc.scalar.activation(xnT[:, H * T + 512 * q:H * T + 512 * q + 512], PS[:, q, :], ACT.Copy)\
                        .then_inc(xnT_ready, 1)
                if norms:
                    for t in range(HT):
                        act.wait_ge(xn_ready, HT * r + t + 1)
                        ins = nc.scalar.activation(sqj[:], xn[:, H * HT + t, :], ACT.Square,
                                                   accum_out=ssq[:, t:t + 1])
                        ins.then_inc(s_act, 1)
                        n_act[0] += 1
                        act.wait_ge(s_act, n_act[0])
                    nc.scalar.activation(nrm[:, H, :], ssq[:], ACT.Sqrt).then_inc(nrm_ready, 1)

            n_act = [1]

            def gates(f):
                act.wait_ge(gd_ready, f + 1)
                nc.scalar.activation(ge[:, f % 2], gd[:, f % 2], ACT.Exp).then_inc(ge_ready, 1)

            def shared(L):
                for q in range(4):
                    for c in range(HC):
                        n = 8 * L + 2 * q + c
                        act.wait_ge(sh_gu, n + 1)
                        if n >= 4:
                            act.wait_ge(sh_h, n - 3)
                        nc.scalar.activation(sil[q % 2][:, c, :], PS[:, 2 + c, :], ACT.Silu).then_inc(sh_sil, 1)

            def experts(L):
                with act.Fori(0, NPAIR // 2) as it:
                    for j in range(2):
                        act.wait_ge(xeT_ps, it * 2 + (NPAIR * L + j + 1))
                        nc.scalar.activation(xeT[j][:], flat(0, 2)[:, 0:PAIR], ACT.Copy).then_inc(xeT_sb, 1)
                        for a in range(2):
                            for c in range(HC):
                                act.wait_ge(gu_ready, it * 8 + (4 * NPAIR * L + 4 * j + 2 * a + c + 1))
                                act.wait_ge(h_ready, it * 8 + (4 * NPAIR * L + 4 * j + 2 * a + c + 1))
                                nc.scalar.activation(sil[a][:, c, 0:CAP], PS[:, 2 + c, 0:CAP], ACT.Silu)\
                                    .then_inc(sil_ready, 1)

            def qk_round(Gi):
                for q, col in ((0, C_SQ), (1, C_SK)):
                    act.wait_ge(qk_ps, 2 * Gi + q + 1)
                    if Gi and q == 0:
                        act.wait_ge(qc_ready, Gi)
                    if Gi and q == 1:
                        act.wait_ge(kz_ready, 16 * HG * Gi)
                    nc.scalar.activation((Qn, Kn)[q][:], flat(2 * q, 2), ACT.Identity,
                                         scale=cst[:, col:col + 1]).then_inc(tq_ready, 1)

            def attention(b):
                for j in range(HT):
                    act.wait_ge(v_ps, HT * b + j + 1)
                    nc.scalar.activation(vs[:, j, 0:8, 0:LAT], PS[:, 2 * (j % 2), :].rearrange("p (h l) -> p h l", l=LAT),
                                         ACT.Copy).then_inc(v_a, 1)
                qk_round(NG * b)
                for g in range(NG):
                    Gi = NG * b + g
                    for n in range(SLOT):
                        N = SLOT * Gi + n
                        if n == 1 and g + 1 < NG:
                            qk_round(Gi + 1)
                        w = CHUNKS[n % NC][2]
                        act.wait_ge(st_ready, N + 1)
                        if N >= 4:
                            act.wait_ge(pv_done, N - 3)
                        nc.scalar.activation(pT[:, N % 4, 0:w], PS[:, 4 + N % 2, 0:w], ACT.Exp).then_inc(exp_done, 1)
                for i in range(HT):
                    n = HT * b + i
                    act.wait_ge(yt_ps, n + 1)
                    if n >= 2:
                        act.wait_ge(wo_ps, n - 1)
                    nc.scalar.activation(yT[i % 2][:, 0:512], PS[:, 2 * (i % 2), :], ACT.Copy).then_inc(yt_a, 1)

            ln(0, 0, True)
            ln(1, 1, True)
            gates(0)
            gates(1)
            shared(0)
            experts(0)
            ln(2, 0, False)
            attention(0)
            ln(3, 0, True)
            gates(2)
            ln(4, 1, False)
            attention(1)
            ln(5, 1, True)
            gates(3)
            shared(1)
            experts(1)

        @block.vector
        def _(dve):
            n_dve = [0]

            def link(ins):
                n_dve[0] += 1
                ins.then_inc(s_dve, 1)
                dve.wait_ge(s_dve, n_dve[0])

            tt, ts, stt = nc.vector.tensor_tensor, nc.vector.tensor_scalar, nc.vector.scalar_tensor_tensor
            nc.vector.memset(wcT[:], 0.0).then_inc(s_zero, 1)
            nc.vector.memset(M[:], 0.0)
            nc.vector.memset(mxp[:], -3.0e38)
            nc.vector.memset(wqx[:], 0.0)
            nc.vector.memset(wkx[:], 0.0)
            nc.vector.memset(bqf[:], 0.0)
            link(nc.vector.memset(bkf[:], 0.0))
            nc.vector.memset(bkf[:, :, 0:R0], 1.0)
            nc.vector.memset(ones2[:].bitcast(F32), 1.0)
            nc.vector.memset(st[:], 0.0).then_inc(in_free, 2)
            nc.vector.memset(mv[:], 0.0).then_inc(h_ready, 2)
            nc.vector.memset(rn[:], 0.0).then_inc(y_sb, 2)
            nc.vector.memset(rec[:], 0.0).then_inc(y_ps, 2)
            nc.vector.memset(gsum[:], 0.0).then_inc(y_out[0], 16)
            nc.vector.memset(mxm[:], 0.0).then_inc(y_out[1], 16)
            dve.wait_ge(s_const, 16)
            nc.vector.tensor_copy(identb[:], ident)
            nc.vector.tensor_copy(trib[:], cst[:, C_TRI:C_TRI + P])
            nc.vector.tensor_copy(onesb[:], cst[:, C_ONE:C_ONE + P])
            nc.vector.tensor_copy(causS[:], cst[:, C_CS:C_CS + P])
            link(nc.vector.tensor_copy(causT[:], cst[:, C_CT:C_CT + P]))
            nc.vector.memset(rstd[:], 0.0).then_inc(s_cst, 1)
            dve.wait_ge(s_cn, 1)
            link(ts(csq[:, 2:3], csq[:, 1:2], 1e-12, None, ALU.max))
            link(nc.vector.reciprocal(csq[:, 3:4], csq[:, 2:3]))
            ts(cenn[:], cen[:], csq[:, 3:4], None, ALU.mult).then_inc(s_cnn, 1)
            dve.wait_ge(s_ct, 1)
            nc.vector.tensor_copy(cenT[:], PS[:, 6, 0:G + E]).then_inc(s_ctc, 1)

            def fold():
                dve.wait_ge(s_w, N_W)
                dve.wait_ge(s_wk, 1)
                for r in range(3):
                    c = slice(R0 + HD * r, R0 + HD * r + HD)
                    ts(wqx[:, :, c], wq_in[:], SCALE, None, ALU.mult)
                    ts(bqf[:, :, c], bq2[:], SCALE, None, ALU.mult)
                    nc.vector.tensor_copy(wkx[:, :, c], PS[:, 6, 0:P].rearrange("p (h d) -> p h d", d=HD))
                    link(nc.vector.tensor_copy(bkf[:, :, c], PS[0:2, 7, 0:P].rearrange("p (h d) -> p h d", d=HD)))
                nc.vector.tensor_copy(brow[:], PS[0:1, 7, P:2 * P])
                for src, dst in ((bqf, bqx), (bkf, bkx)):
                    f = src[:].rearrange("p h r -> p (h r)")
                    link(ts(bqs[:].bitcast(F32R), f, cst[0:2, C_S2:C_S2 + 1], None, ALU.mult))
                    link(stt(dst[:], f, cst[0:2, C_L2:C_L2 + 1], bqs[:], ALU.mult, ALU.add))
                nc.vector.memset(rstd[:], 0.0).then_inc(s_ax, 1)

            def ln(r, H):
                t0 = H * HT
                for t in range(HT):
                    ins = nc.vector.bn_stats(st[:, t, :], xs[:, t0 + t, :])
                link(ins)
                for t in range(HT):
                    ins = nc.vector.bn_aggr(mv[:, t, :], st[:, t, :])
                ins.then_inc(ln_stat, 1)
                dve.wait_ge(ln_std, r + 1)
                link(nc.vector.reciprocal(rstd[:], std[:]))
                if r >= 2:
                    dve.wait_ge(scat, 32 * 16 * {2: 1, 3: 1, 4: 2, 5: 2}[r])
                for t in range(HT):
                    ts(xn[:, t0 + t, :], xs[:, t0 + t, :], mv[:, t, 0:1], rstd[:, t:t + 1], ALU.subtract, ALU.mult)\
                        .then_inc(xn_ready, 1)

            def route(f, H):
                dve.wait_ge(nrm_ready, f + 1)
                link(ts(rn[:], nrm[:, H, :], 1e-12, None, ALU.max))
                link(nc.vector.reciprocal(rn[:], rn[:]))
                dve.wait_ge(sc_ready, f + 1)
                sc = PS[:, 6, 0:HT * (G + E)].rearrange("p (t n) -> p t n", n=G + E)
                tt(gs[:], sc[:, :, 0:G], rn[:].unsqueeze(2).broadcast_to([P, HT, G]), ALU.mult)
                link(tt(es[:], sc[:, :, G:G + E], rn[:].unsqueeze(2).broadcast_to([P, HT, E]), ALU.mult))
                link(tt(es[:], es[:], ebb[:].unsqueeze(1).broadcast_to([P, HT, E]), ALU.add))
                for t in range(HT):
                    ins = nc.vector.max(v8[:, t, :], gs[:, t, :])
                link(ins)
                for t in range(HT):
                    ins = nc.vector.max_index(i8[:, t, :], v8[:, t, :], gs[:, t, :])
                link(ins)
                link(nc.vector.tensor_copy(idf[:], i8[:, :, 0:KG]))
                link(tt(geq[:], cst[:, C_I8:C_I8 + G].unsqueeze(1).broadcast_to([P, HT * KG, G]),
                        idf[:].rearrange("p t k -> p (t k)").unsqueeze(2).broadcast_to([P, HT * KG, G]), ALU.is_equal))
                link(nc.vector.tensor_reduce(gm[:], geq[:].rearrange("p (t k) g -> p t g k", k=KG), AX.X, ALU.add))
                ts(pen[:], gm[:], 1.0e9, -1.0e9, ALU.mult, ALU.add)
                gmf = gm[:].rearrange("p t g -> p (t g)").unsqueeze(2).broadcast_to([P, HT * G, EG])
                pnf = pen[:].rearrange("p t g -> p (t g)").unsqueeze(2).broadcast_to([P, HT * G, EG])
                mkf = mk[:].rearrange("p t (g e) -> p (t g) e", e=EG)
                link(tt(mkf, es[:].rearrange("p t (g e) -> p (t g) e", e=EG), gmf, ALU.mult))
                link(tt(mkf, mkf, pnf, ALU.add))
                for t in range(HT):
                    ins = nc.vector.max(v8[:, t, :], mk[:, t, :])
                link(ins)
                tt(gd[:, H], v8[:, :, 0:K], v8[:, :, 0:1].broadcast_to([P, HT, K]), ALU.subtract).then_inc(gd_ready, 1)
                for t in range(HT):
                    ins = nc.vector.max_index(i8[:, t, :], v8[:, t, :], mk[:, t, :])
                link(ins)
                link(nc.vector.tensor_copy(eif[:], i8[:, :, 0:K]))
                link(tt(oh[:], cst[:, C_I32:C_I32 + E].unsqueeze(1).broadcast_to([P, HT * K, E]),
                        eif[:].rearrange("p t k -> p (t k)").unsqueeze(2).broadcast_to([P, HT * K, E]), ALU.is_equal))
                with nc.allow_low_precision("zeros and ones"):
                    nc.vector.tensor_reduce(sel[:, H * HT:H * HT + HT, :], oh[:].rearrange("p (t k) e -> p t e k", k=K),
                                            AX.X, ALU.add).then_inc(sel_ready, 1)
                dve.wait_ge(ge_ready, f + 1)
                link(nc.vector.tensor_reduce(gsum[:], ge[:, H], AX.X, ALU.add))
                link(nc.vector.reciprocal(gsum[:], gsum[:]))
                tt(ge[:, H], ge[:, H], gsum[:].unsqueeze(2).broadcast_to([P, HT, K]), ALU.mult)
                dve.wait_ge(cum_ready, f + 1)
                cnt = PS[:, 7, H * HT * E:(H + 1) * HT * E].rearrange("p (t e) -> p t e", e=E)
                link(tt(pc[:].rearrange("p (t k) e -> p t k e", k=K), oh[:].rearrange("p (t k) e -> p t k e", k=K),
                        cnt.unsqueeze(2).broadcast_to([P, HT, K, E]), ALU.mult))
                link(nc.vector.tensor_reduce(pos[:], pc[:], AX.X, ALU.add))
                ts(over[:], pos[:], float(CAP), float(SKIP), ALU.is_gt, ALU.mult)
                ts(keep[:], pos[:], float(CAP), 0.5, ALU.is_le, ALU.mult)
                link(ts(pos[:], pos[:], float(CAP), -1.0, ALU.min, ALU.add))
                link(stt(slf[:], eif[:].rearrange("p t k -> p (t k)"), float(CAP), pos[:], ALU.mult, ALU.add))
                nc.vector.tensor_copy(gidx[:, H, :], slf[:])
                link(tt(gate[:, H, :], ge[:, H].rearrange("p t k -> p (t k)"), keep[:], ALU.mult))
                tt(sidx[:, H, :], slf[:], over[:], ALU.add).then_inc(slot_ready, 1)

            def shared(L):
                for q in range(4):
                    for c in range(HC):
                        n = 8 * L + 2 * q + c
                        dve.wait_ge(sh_sil, n + 1)
                        if n >= 4:
                            dve.wait_ge(sh_y, (n - 4) // 2 + 1)
                        tt(hb[q % 2][:, c, :], sil[q % 2][:, c, :], PS[:, 4 + c, :], ALU.mult).then_inc(sh_h, 1)
                    if q:
                        shared_x(L, q - 1)
                shared_x(L, 3)

            def shared_x(L, q):
                dve.wait_ge(sh_y, 4 * L + q + 1)
                xq = xs[:, 4 * q:4 * q + 4, :].rearrange("p t d -> p (t d)")
                stt(xq, PS[:, 6 + q % 2, :], 0.5, xq, ALU.mult, ALU.add).then_inc(sh_x, 1)

            def experts(L):
                with dve.Fori(0, NPAIR // 2) as it:
                    for j in range(2):
                        for a in range(2):
                            for c in range(HC):
                                dve.wait_ge(sil_ready, it * 8 + (4 * NPAIR * L + 4 * j + 2 * a + c + 1))
                                if c == 0:
                                    dve.wait_ge(y_ps, it * 4 + (2 * NPAIR * L + 2 * j + a) + 1)
                                tt(hb[a][:, c, 0:CAP], sil[a][:, c, 0:CAP], PS[:, 4 + c, 0:CAP], ALU.mult)\
                                    .then_inc(h_ready, 1)
                        dve.wait_ge(y_out[j], it * 16 + (16 * NPAIR // 2 * L + 16))
                        for a in range(2):
                            dve.wait_ge(y_ps, it * 4 + (2 * NPAIR * L + 2 * j + a + 3))
                            ya = PS[:, 6 + a, 0:3 * D].rearrange("p (t d) -> p t d", d=D)
                            if a == 0:
                                nc.vector.tensor_copy(yo[j][:, 0:2, :], ya[:, 0:2, :])
                                nc.vector.tensor_copy(yo[j][0:64, 2, :], ya[0:64, 2, :]).then_inc(y_sb, 1)
                            else:
                                nc.vector.tensor_copy(yo[j][64:P, 2, :], ya[64:P, 0, :])
                                nc.vector.tensor_copy(yo[j][:, 3:5, :], ya[:, 1:3, :]).then_inc(y_sb, 1)

            def combine(L, H):
                for t in range(HT):
                    dve.wait_ge(gath[t], 16 * K * (2 * L + H + 1))
                    xt = xs[:, H * HT + t, :]
                    for k in range(K):
                        ins = stt(xt, yg[:, t, k, :], gate[:, H, t * K + k:t * K + k + 1], xt, ALU.mult, ALU.add)
                        if k < K - 1:
                            link(ins)
                    ins.then_inc(comb, 1)
                dve.wait_ge(comb, HT * (2 * L + H + 1))

            def qk_parts(Gi):
                for q, (dst, col) in enumerate(((Qn, C_LQ), (Kn, C_LK))):
                    dve.wait_ge(tq_ready, 2 * Gi + q + 1)
                    stt(dst[:], flat(2 * q, 2), cst[:, col:col + 1], dst[:].bitcast(F32), ALU.mult, ALU.add)\
                        .then_inc(qk_split, 1)

            def row_max(Gi, s):
                i, c, w = ROWS[s // 2]
                hp = s % 2
                dve.wait_ge(s_ready, NS * Gi + s + 1)
                nc.vector.tensor_reduce(mxp[:, i, c, 2 * hp:2 * hp + 2], PS[:, 2 * hp:2 * hp + 2, 0:w], AX.X, ALU.max)\
                    .then_inc(smax, 1)

            def max_parts(Gi):
                dve.wait_ge(smax, NS * Gi + NS)
                link(tt(mxm[:], mxp[:, :, 0, :], mxp[:, :, 1, :], ALU.max))
                if Gi:
                    dve.wait_ge(mt_ready, Gi)
                link(ts(M[:, :, :, 0].bitcast(F32R), mxm[:], -1.0, None, ALU.mult))
                stt(M[:, :, :, 1].bitcast(F32R), mxm[:], -1.0, M[:, :, :, 0], ALU.mult, ALU.subtract)\
                    .then_inc(m_ready, 1)

            def q_with_max(Gi):
                dve.wait_ge(mt_ready, Gi + 1)
                tt(Qc[Gi % 2][:], flat(0, 2), Qn[:].bitcast(F32), ALU.add).then_inc(qc_ready, 1)

            def normalise(Gi, hh, half):
                X = HG * Gi + hh
                dve.wait_ge(pv_done, SLOT * Gi + NC * hh + (4 if half == 0 else NC))
                o = PS[:, 6 + half, :].rearrange("p (t l) -> p t l", l=P)
                link(nc.vector.reciprocal(rec[:, half], o[:, :, LAT:VW]))
                h = (Gi % NG) * HG + hh
                tt(os_[:, 4 * half:4 * half + 4, h * LAT:(h + 1) * LAT], o[:, :, 0:LAT],
                   rec[:, half].broadcast_to([P, 4, LAT]), ALU.mult).then_inc(norm_done, 1)

            def attention(b):
                nc.vector.memset(area_v[:, HT * NH * VW:], 0.0)
                nc.vector.memset(vs[:, :, :, LAT:VW], 1.0)
                for j in range(HT):
                    dve.wait_ge(v_ps, HT * b + j + 1)
                    nc.vector.tensor_copy(vs[:, j, 8:16, 0:LAT],
                                          PS[:, 2 * (j % 2) + 1, :].rearrange("p (h l) -> p h l", l=LAT)).then_inc(v_d, 1)
                qk_parts(NG * b)
                for s in range(NS):
                    row_max(NG * b, s)
                max_parts(NG * b)
                q_with_max(NG * b)
                for g in range(NG):
                    Gi = NG * b + g
                    for n in range(SLOT):
                        if n % NC == 6:
                            normalise(Gi, n // NC, 0)
                        if n % NC == 2 and n > NC:
                            normalise(Gi, n // NC - 1, 1)
                        if g + 1 < NG:
                            if n == 2:
                                qk_parts(Gi + 1)
                            for s in s_steps_at(n):
                                row_max(Gi + 1, s)
                            if n == 36:
                                max_parts(Gi + 1)
                            if n == 39:
                                q_with_max(Gi + 1)
                    normalise(Gi, HG - 1, 1)
                for i in range(HT):
                    n = HT * b + i
                    dve.wait_ge(yt_ps, n + 1)
                    if n >= 2:
                        dve.wait_ge(wo_ps, n - 1)
                    nc.vector.tensor_copy(yT[i % 2][:, 512:1024], PS[:, 2 * (i % 2) + 1, :]).then_inc(yt_d, 1)
                    if i:
                        add_x(b, i - 1)
                add_x(b, HT - 1)
                dve.wait_ge(wo_x, HT * (b + 1))

            def add_x(b, i):
                dve.wait_ge(wo_ps, HT * b + i + 1)
                xt = xs[:, HT * b + i, :]
                tt(xt, PS[:, 6 + i % 2, 0:D], xt, ALU.add).then_inc(wo_x, 1)

            dve.wait_ge(s_x, 64)
            ln(0, 0)
            ln(1, 1)
            route(0, 0)
            route(1, 1)
            fold()
            shared(0)
            experts(0)
            combine(0, 0)
            ln(2, 0)
            attention(0)
            combine(0, 1)
            ln(3, 0)
            route(2, 0)
            ln(4, 1)
            attention(1)
            ln(5, 1)
            route(3, 1)
            shared(1)
            experts(1)
            combine(1, 0)
            combine(1, 1)

        @block.tensor
        def _(pe):
            mm = nc.tensor.matmul

            def ln(r, H):
                for q in range(2):
                    for t in range(4):
                        tile = 4 * q + t
                        pe.wait_ge(xn_ready, HT * r + tile + 1)
                        ins = nc.tensor.transpose(PS[:, q, t * P:(t + 1) * P], xn[:, H * HT + tile, :], ident)
                    ins.then_inc(xnT_ps, 1)

            def scores(r, H):
                pe.wait_ge(xnT_ready, 2 * r + 2)
                for t in range(HT):
                    c0 = (H * HT + t) * P
                    ins = mm(PS[:, 6, t * (G + E):(t + 1) * (G + E)], xnT[:, c0:c0 + P], cenT[:], start=True, stop=True)
                ins.then_inc(sc_ready, 1)

            def counts(f, H):
                pe.wait_ge(sel_ready, f + 1)
                t0, t1 = H * HT, H * HT + HT
                def cols(a, b):
                    return PS[:, 7, a * E:b * E]
                for j in range(t1 - 1):
                    a = max(j + 1, t0)
                    mm(cols(a, t1).rearrange("p (t e) -> p t e", e=E), onesb[:],
                       sel[:, j:j + 1, :].broadcast_to([P, t1 - a, E]), start=(j == 0), stop=False, skip_group_check=True)
                mm(cols(t0, t1), trib[:], sel[:, t0:t1, :].rearrange("p t e -> p (t e)"), start=False, stop=True,
                   skip_group_check=True).then_inc(cum_ready, 1)

            def shared(L):
                def down(q):
                    pe.wait_ge(sh_h, 8 * L + 2 * q + 2)
                    if q >= 2:
                        pe.wait_ge(sh_x, 4 * L + q - 1)
                    for c in range(HC):
                        for t in range(4):
                            ins = mm(PS[:, 6 + q % 2, t * D:(t + 1) * D], hb[q % 2][:, c, t * P:(t + 1) * P], sdw[:, c, :],
                                     start=(c == 0 and t == 0), stop=(c == HC - 1), skip_group_check=True)
                    ins.then_inc(sh_y, 1)

                for q in range(4):
                    for c in range(HC):
                        n = 8 * L + 2 * q + c
                        if q:
                            pe.wait_ge(sh_h, n - 1)
                        rhs = xnT[:, 512 * q:512 * q + 512]
                        mm(PS[:, 2 + c, :], sgw[:, c * P:(c + 1) * P], rhs, start=True, stop=True)
                        mm(PS[:, 4 + c, :], suw[:, c * P:(c + 1) * P], rhs, start=True, stop=True).then_inc(sh_gu, 1)
                    if q:
                        down(q - 1)
                down(3)

            def experts(L):
                pe.wait_ge(sh_x, 4 * L + 4)
                with pe.Fori(0, NPAIR // 2) as it:
                    for j in range(2):
                        pe.wait_ge(x_in[j], it * 16 + (16 * NPAIR // 2 * L + 16))
                        for t in range(PT):
                            ins = nc.tensor.transpose(flat(0, 2)[:, t * P:(t + 1) * P], xe[j][:, t, :], ident)
                        ins.then_inc(xeT_ps, 1)
                        pe.wait_ge(w_in[j], it * 64 + (64 * NPAIR // 2 * L + 64))
                        pe.wait_ge(xeT_sb, it * 2 + (NPAIR * L + j + 1))
                        for a in range(2):
                            gate_up(L, it, j, a)
                            if a:
                                down(L, it, j, 0)
                        down(L, it, j, 1)

            def gate_up(L, it, j, a):
                rhs = xeT[j][:, a * CAP:(a + 1) * CAP]
                for c in range(HC):
                    pe.wait_ge(h_ready, it * 8 + (4 * NPAIR * L + 4 * j + 2 * a + c + 1))
                    mm(PS[:, 2 + c, 0:CAP], wgt[j][:, a, c * P:(c + 1) * P], rhs, start=True, stop=True)
                    mm(PS[:, 4 + c, 0:CAP], wut[j][:, a, c * P:(c + 1) * P], rhs, start=True, stop=True)\
                        .then_inc(gu_ready, 1)

            def down(L, it, j, a):
                pe.wait_ge(y_sb, it * 4 + (2 * NPAIR * L + 2 * j + a + 1))
                tiles = ((0, P, 0, 0), (P, P, 0, 1), (2 * P, 64, 0, 2)) if a == 0 else \
                    ((64, P, 0, 1), (64 + P, P, 0, 2), (0, 64, 64, 0))
                for c in range(HC):
                    pe.wait_ge(h_ready, it * 8 + (4 * NPAIR * L + 4 * j + 2 * a + c + 3))
                    for n, (col, m, p0, t) in enumerate(tiles):
                        ins = mm(PS[p0:p0 + m, 6 + a, t * D:(t + 1) * D], hb[a][:, c, col:col + m], wdt[j][:, a, c, :],
                                 start=(c == 0 and n == 0) , stop=(c == HC - 1), skip_group_check=True)
                if a:
                    ins.then_inc(y_ps, 1)
                    nc.tensor.matmul(PS[0:1, 0, 0:1], onesb[:, 0:1], onesb[:, 0:1], start=True, stop=True)\
                        .then_inc(in_free, 1)
                else:
                    ins.then_inc(y_ps, 1)

            def values(b):
                for j in range(HT):
                    if j >= 2:
                        pe.wait_ge(v_a, HT * b + j - 1)
                        pe.wait_ge(v_d, HT * b + j - 1)
                    for c in range(2):
                        ins = mm(PS[:, 2 * (j % 2) + c, :], xnT[:, (HT * b + j) * P:(HT * b + j + 1) * P],
                                 wv_in[:, 512 * c:512 * c + 512], start=True, stop=True)
                    ins.then_inc(v_ps, 1)
                pe.wait_ge(v_a, HT * (b + 1))
                pe.wait_ge(v_d, HT * (b + 1))

            def qk(Gi):
                b, g = Gi // NG, Gi % NG
                if Gi % NG:
                    pe.wait_ge(qc_ready, Gi)
                gc = slice(g * HG * RW, (g + 1) * HG * RW)
                for q, (w, bias) in enumerate(((wqx, bqx), (wkx, bkx))):
                    for c in range(2):
                        o = PS[:, 2 * q + c, :]
                        mm(o, w[:].rearrange("p h r -> p (h r)")[:, gc], xnT[:, b * T + 512 * c:b * T + 512 * c + 512],
                           start=True, stop=False)
                        ins = mm(o, bias[:, gc], ones2[:], start=False, stop=True)
                    ins.then_inc(qk_ps, 1)

            def s_rows(Gi, s):
                i, c, w = ROWS[s // 2]
                hp = s % 2
                if s == 0:
                    pe.wait_ge(qk_split, 2 * Gi + 2)
                    pe.wait_ge(kz_ready, 16 * HG * (Gi + 1))
                if s >= 2:
                    pe.wait_ge(smax, NS * Gi + s - 1)
                diag = c == i // 4
                for hh in range(2):
                    o = PS[:, 2 * hp + hh, 0:w]
                    ins = mm(o, Qn[:, i * P:(i + 1) * P], Kz[Gi % 2][:, 2 * hp + hh, 512 * c:512 * c + w],
                             start=True, stop=not diag)
                    if diag:
                        ins = mm(o[:, w - P:w], identb[:], causS[:], start=False, stop=True)
                ins.then_inc(s_ready, 1)

            def max_rows(Gi):
                pe.wait_ge(m_ready, Gi + 1)
                for i in range(HT):
                    ins = nc.tensor.transpose(flat(0, 2)[:, i * P:(i + 1) * P], M[:, i].rearrange("p h r -> p (h r)"), ident)
                ins.then_inc(mt_ready, 1)

            def s_cols(Gi, n):
                N = SLOT * Gi + n
                j, t0, w, _ = CHUNKS[n % NC]
                if N >= 2:
                    pe.wait_ge(exp_done, N - 1)
                diag = t0 == j * P
                o = PS[:, 4 + N % 2, 0:w]
                ins = mm(o, Kz[Gi % 2][:, n // NC, j * P:(j + 1) * P], Qc[Gi % 2][:, t0:t0 + w], start=True, stop=not diag)
                if diag:
                    ins = mm(o[:, 0:P], identb[:], causT[:], start=False, stop=True)
                ins.then_inc(st_ready, 1)

            def pv(Gi, n):
                N = SLOT * Gi + n
                j, t0, w, half = CHUNKS[n % NC]
                X = HG * Gi + n // NC
                first = n % NC == (0 if half == 0 else 4)
                if first and X:
                    pe.wait_ge(norm_done, 2 * X - 1 + half)
                pe.wait_ge(exp_done, N + 1)
                h = (Gi % NG) * HG + n // NC
                for k in range(w // P):
                    i = t0 // P + k
                    ins = mm(PS[:, 6 + half, (i % 4) * P:(i % 4 + 1) * P], pT[:, N % 4, k * P:(k + 1) * P],
                             area_v[:, (j * NH + h) * VW:(j * NH + h) * VW + P],
                             start=(first and k == 0), stop=(i == j), skip_group_check=True)
                ins.then_inc(pv_done, 1)

            def attention(b):
                values(b)
                qk(NG * b)
                for s in range(NS):
                    s_rows(NG * b, s)
                max_rows(NG * b)
                for g in range(NG):
                    Gi = NG * b + g
                    pe.wait_ge(qc_ready, Gi + 1)
                    for n in range(SLOT):
                        s_cols(Gi, n)
                        if n >= 2:
                            pv(Gi, n - 2)
                        if g + 1 < NG:
                            if n == 0:
                                qk(Gi + 1)
                            for s in s_steps_at(n):
                                s_rows(Gi + 1, s)
                            if n == 38:
                                max_rows(Gi + 1)
                    pv(Gi, SLOT - 2)
                    pv(Gi, SLOT - 1)
                pe.wait_ge(norm_done, 2 * NH * (b + 1))
                for i in range(HT):
                    n = HT * b + i
                    if i >= 2:
                        pe.wait_ge(yt_a, n - 1)
                        pe.wait_ge(yt_d, n - 1)
                    for c in range(8):
                        ins = nc.tensor.transpose(flat(2 * (i % 2), 2)[:, c * P:(c + 1) * P], os_[:, i, c * P:(c + 1) * P], ident)
                    ins.then_inc(yt_ps, 1)
                    if i:
                        out_proj(b, i - 1)
                out_proj(b, HT - 1)
                pe.wait_ge(wo_x, HT * (b + 1))

            def out_proj(b, i):
                n = HT * b + i
                pe.wait_ge(yt_a, n + 1)
                pe.wait_ge(yt_d, n + 1)
                if i >= 2:
                    pe.wait_ge(wo_x, n - 1)
                o = PS[:, 6 + i % 2, 0:D]
                mm(o, cst[0:1, C_ONE:C_ONE + P], brow[:], start=True, stop=False)
                for c in range(8):
                    ins = mm(o, yT[i % 2][:, c * P:(c + 1) * P], wo_in[:, c, :], start=False, stop=(c == 7))
                ins.then_inc(wo_ps, 1)

            pe.wait_ge(s_const, 16)
            pe.wait_ge(s_cst, 1)
            pe.wait_ge(s_cnn, 1)
            nc.tensor.transpose(PS[:, 6, 0:G + E], cenn[:], ident[0:G + E, 0:G + E]).then_inc(s_ct, 1)
            pe.wait_ge(s_w, N_W)
            pe.wait_ge(s_ctc, 1)
            ln(0, 0)
            scores(0, 0)
            ln(1, 1)
            pe.wait_ge(sel_ready, 1)
            scores(1, 1)
            counts(0, 0)
            counts(1, 1)
            pe.wait_ge(slot_ready, 2)
            wc2 = wcT[:].rearrange("p a d -> p (a d)")
            for c in range(8):
                mm(PS[:, 6, c * 2 * HD:(c + 1) * 2 * HD], wkT[:, c * P:(c + 1) * P], wc2, start=True, stop=True)
                mm(PS[0:2, 7, c * 2 * HD:(c + 1) * 2 * HD], bk2[:, c, :], wc2, start=True, stop=True)
            mm(PS[0:1, 7, P:2 * P], cst[0:1, C_ONE:C_ONE + 1], bor[:], start=True, stop=False)
            for c in range(8):
                ins = mm(PS[0:1, 7, P:2 * P], bvc[:, c:c + 1], wo_in[:, c, :], start=False, stop=(c == 7))
            ins.then_inc(s_wk, 1)
            pe.wait_ge(s_ax, 1)
            shared(0)
            experts(0)
            ln(2, 0)
            pe.wait_ge(xnT_ready, 6)
            attention(0)
            ln(3, 0)
            scores(3, 0)
            counts(2, 0)
            pe.wait_ge(xnT_ready, 8)
            pe.wait_ge(slot_ready, 3)
            ln(4, 1)
            pe.wait_ge(xnT_ready, 10)
            attention(1)
            ln(5, 1)
            scores(5, 1)
            counts(3, 1)
            pe.wait_ge(slot_ready, 4)
            shared(1)
            experts(1)


_INS = ['L0_attn_x', 'L0_attn_Wq', 'L0_attn_bq', 'L0_attn_Wk', 'L0_attn_bk', 'L0_attn_Wv', 'L0_attn_bv', 'L0_attn_Wo',
        'L0_attn_bo', 'L0_attn_Wc', 'L0_ffn_group_centroids', 'L0_ffn_expert_centroids', 'L0_ffn_bias', 'L0_ffn_wg',
        'L0_ffn_wu', 'L0_ffn_wd', 'L0_ffn_sg', 'L0_ffn_su', 'L0_ffn_sd']


def shape_constants():
    import numpy as np
    c = np.zeros((P, C_N), np.float32)
    p, q = np.arange(P)[:, None], np.arange(P)[None, :]
    c[:, C_ID:C_ID + P] = p == q
    c[:, C_TRI:C_TRI + P] = p <= q
    c[:, C_CS:C_CS + P] = np.where(q > p, NEG, 0.0)
    c[:, C_CT:C_CT + P] = np.where(p > q, NEG, 0.0)
    c[:, C_I8:C_I8 + G] = np.arange(G)
    c[:, C_I32:C_I32 + E] = np.arange(E)
    r = np.arange(P) % RW
    lo_q = (r >= R0 + 2 * HD) & (r < R0 + 3 * HD)
    lo_k = (r >= R0 + HD) & (r < R0 + 2 * HD)
    lo_2 = np.arange(P) == 1
    for lo, s, l in ((lo_q, C_SQ, C_LQ), (lo_k, C_SK, C_LK), (lo_2, C_S2, C_L2)):
        c[:, s] = np.where(lo, -1.0, 1.0)
        c[:, l] = lo
    c[:, C_EPS] = 1e-5
    c[:, C_ONE:C_ONE + P] = 1.0
    return c


def layouts(inputs):
    import numpy as np
    a = {n: np.asarray(inputs[n]) for n in _INS[1:10]}
    pairs = NH * LAT // P
    return {
        'L0_attn_bq': np.stack([a['L0_attn_bq']] * 2),
        'L0_attn_Wk': a['L0_attn_Wk'].T.reshape(pairs, P, D).transpose(1, 0, 2).reshape(P, -1),
        'L0_attn_bk': np.stack([a['L0_attn_bk'].reshape(pairs, P).T] * 2, axis=2),
        'L0_attn_bv': a['L0_attn_bv'].reshape(pairs, P).T,
        'L0_attn_Wc': a['L0_attn_Wc'].T,
    }


def kernel(**inputs):
    import numpy as _np
    import concourse.bacc as _bacc
    from concourse import mybir as _mybir
    from concourse.bass_utils import run_bass_kernel_spmd as _run

    nc = _bacc.Bacc("TRN2", target_bir_lowering=False, num_devices=1)
    arrays, args = {}, []
    laid = layouts(inputs)
    for name in _INS:
        a = _np.ascontiguousarray(laid.get(name, inputs[name]))
        arrays[f"in_{name}_dram"] = a
        args.append(nc.dram_tensor(f"in_{name}_dram", a.shape, _mybir.dt.from_np(a.dtype), kind="ExternalInput").ap())
    arrays["in_consts_dram"] = shape_constants()
    args.append(nc.dram_tensor("in_consts_dram", (P, C_N), _mybir.dt.float32, kind="ExternalInput").ap())
    args.append(nc.dram_tensor("out_0_dram", (B, T, D), _mybir.dt.float32, kind="ExternalOutput").ap())
    program(nc, *args)
    r = _run(nc, [arrays], core_ids=[0])
    return r.results[0]["out_0_dram"]
```

```python
from contextlib import ExitStack

import concourse.bass as bass
from concourse import mybir

F32 = mybir.dt.float32
F32R = mybir.dt.float32r
BF16 = mybir.dt.bfloat16
U32 = mybir.dt.uint32
I32 = mybir.dt.int32
ALU = mybir.AluOpType
ACT = mybir.ActivationFunctionType
AX = mybir.AxisListType

P = 128
B, T, D = 2, 1024, 128
NT = B * T // P
HT = T // P
E, G, K = 32, 8, 4
EG = E // G
KG = G // 2
HID = 256
HC = HID // P
CAP = int(B * T / E * K * 1.25)
PAIR = 2 * CAP
PT = PAIR // P
NPAIR = E // 2
SLOTS = E * CAP
SKIP = 2 * SLOTS
DX = D + 8
X_TOK, X_EXP = D, D + 1
RES = K * B * T
LAYER = 2 * RES
NH, LAT, HD = 16, 64, 8
HG = 4
NG = NH // HG
RW = 32
R0 = 2
VW = LAT + 1
SCALE = 1.0 / 8.0
NEG = -1.0e30

C_ID, C_TRI, C_CS, C_CT, C_I8, C_I32 = 0, 128, 256, 384, 512, 520
C_SQ, C_LQ, C_SK, C_LK, C_S2, C_L2, C_EPS, C_ONE = 552, 553, 554, 555, 556, 557, 558, 560
C_TOK, C_EID, C_K, C_N = 688, 704, 709, 713

ROWS = [(i, c, min(512, (i + 1) * P) if c == 0 else (i - 3) * P) for i in range(HT) for c in range(1 + i // 4)]
NS = 2 * len(ROWS)
CHUNKS = [(j, j * P, 512 - j * P, 0) for j in range(4)] + \
         [(j, max(512, j * P), 1024 - max(512, j * P), 1) for j in range(8)]
NC = len(CHUNKS)
SLOT = HG * NC


AT_QK, AT_SPLIT, AT_LN, AT_TR, AT_SC, AT_READ, AT_CNT, AT_S0 = 0, 2, 3, 10, 14, 16, 16, 18
AT_MAX, AT_MT, AT_QC = AT_S0 + NS, AT_S0 + NS + 2, AT_S0 + NS + 3
G_COMB, G_LN1, G_LN0, G_ROUTE = 0, 1, NG, NG + 1


def score_bank(f):
    return 2 if f == 2 else 6


def program(nc, x, Wq, bq, WkT, bk, Wv, bv, Wo, bo, WcT, gcen, ecen, ebias, wg, wu, wd, sg, su, sd, consts, out):
    xbuf = nc.dram_tensor("xbuf", [SLOTS, DX], F32).ap()
    ybuf = nc.dram_tensor("ybuf", [RES, D], F32).ap()
    x_t = x.rearrange("b (n p) d -> p (b n) d", p=P)
    out_t = out.rearrange("b (n p) d -> p (b n) d", p=P)

    with ExitStack() as ctx:
        def sb(name, shape, dt=F32):
            return ctx.enter_context(nc.sbuf_tensor(name, shape, dt))

        def sem(name):
            return ctx.enter_context(nc.semaphore(name))

        PS = ctx.enter_context(nc.psum_tensor("PS", [P, 8, 512], F32))

        def flat(b0, n):
            return PS[:, b0:b0 + n, :].rearrange("p b n -> p (b n)")

        cst = sb("cst", [P, C_N])
        identb = sb("identb", [P, P], BF16)
        trib = sb("trib", [P, P], BF16)
        onesb = sb("onesb", [P, P], BF16)
        causS = sb("causS", [P, P], BF16)
        causT = sb("causT", [P, P], BF16)
        xs = sb("xs", [P, NT, D])
        xn = sb("xn", [P, NT, DX])
        xnT = sb("xnT", [P, NT * P])
        cen = sb("cen", [G + E, D])
        cenn = sb("cenn", [G + E, D])
        cenT = sb("cenT", [P, G + E])
        csq = sb("csq", [G + E, 4])
        ebb = sb("ebb", [P, E])
        st = sb("st", [P, HT, 6])
        mv = sb("mv", [P, HT, 2])
        std = sb("std", [P, HT])
        rstd = sb("rstd", [P, HT])
        sqj = sb("sqj", [P, D])
        ssq = sb("ssq", [P, HT])
        nrm = sb("nrm", [P, 2, HT])
        rn = sb("rn", [P, HT])
        gs = sb("gs", [P, HT, G])
        es = sb("es", [P, HT, E])
        v8 = sb("v8", [P, HT, 8])
        i8 = sb("i8", [P, HT, 8], U32)
        idf = sb("idf", [P, HT, K])
        eif = sb("eif", [P, HT, K])
        gm = sb("gm", [P, HT, G])
        pen = sb("pen", [P, HT, G])
        mk = sb("mk", [P, HT, E])
        sel = sb("sel", [P, NT, E], BF16)
        gd = sb("gd", [P, 2, HT, K])
        ge = sb("ge", [P, 2, HT, K])
        gsum = sb("gsum", [P, HT])
        pos = sb("pos", [P, HT * K])
        over = sb("over", [P, HT * K])
        keep = sb("keep", [P, HT * K])
        slf = sb("slf", [P, HT * K])
        gate = sb("gate", [P, 2, HT * K])
        sidx = sb("sidx", [P, 2, HT * K], I32)
        eid = sb("eid", [P, PT])
        hit = sb("hit", [P, PT, K])
        kth = sb("kth", [P, PT])
        yidx = sb("yidx", [P, 2, PT], I32)
        sgw = sb("sgw", [P, HID])
        suw = sb("suw", [P, HID])
        sdw = sb("sdw", [P, HC, D])
        yg = sb("yg", [P, HT, K, D])
        wq_in = sb("wq_in", [P, NH, HD])
        wv_in = sb("wv_in", [P, NH * LAT])
        wo_in = sb("wo_in", [P, 8, D])
        wcT = sb("wcT", [P, 2, HD])
        bk2 = sb("bk2", [P, 8, 2])
        bvc = sb("bvc", [P, 8])
        bor = sb("bor", [1, D])
        brow = sb("brow", [1, D])
        bq2 = sb("bq2", [2, NH, HD])
        wqx = sb("wqx", [P, NH, RW])
        wkx = sb("wkx", [P, NH, RW])
        bqf = sb("bqf", [2, NH, RW])
        bkf = sb("bkf", [2, NH, RW])
        bqs = sb("bqs", [2, NH * RW])
        bqx = sb("bqx", [2, NH * RW], F32R)
        bkx = sb("bkx", [2, NH * RW], F32R)
        ones2 = sb("ones2", [2, 512], F32R)
        Qn = sb("Qn", [P, T], F32R)
        Kn = sb("Kn", [P, T], F32R)
        Qc = [sb(f"Qc{i}", [P, T], F32R) for i in range(2)]
        Kz = [sb(f"Kz{i}", [P, HG, T], F32R) for i in range(2)]
        mxp = sb("mxp", [P, HT, 2, HG])
        mxm = sb("mxm", [P, HT, HG])
        M = sb("M", [P, HT, HG, RW])
        pT = sb("pT", [P, 4, 512])
        rec = sb("rec", [P, 2, 4, 1])
        area_o = sb("area_o", [P, HT * NH * LAT])
        area_v = sb("area_v", [P, HT * NH * VW + P - VW])

        def parts(area, first, *shapes):
            views, at = [], first
            for shape, pattern, sizes in shapes:
                v = area[:, at:at + shape]
                views.append(v.rearrange(pattern, **sizes) if pattern else v)
                at += shape
            assert at <= area.shape[1]
            return views

        os_ = area_o[:].rearrange("p (i n) -> p i n", i=HT)
        vs = area_v[:, 0:HT * NH * VW].rearrange("p (j h l) -> p j h l", j=HT, h=NH)
        half = ("p (c n) -> p c n", dict(c=HC))
        sil0, sil1, hb0, hb1 = parts(area_o, 0, *[(HC * 512, *half)] * 4)
        sil, hb = [sil0, sil1], [hb0, hb1]
        xeT0, xeT1 = parts(area_o, 4 * HC * 512, *[(PAIR, None, None)] * 2)
        xeT = [xeT0, xeT1]
        rows = (PAIR, "p (t d) -> p t d", dict(d=D))
        xrows = (PT * DX, "p (t d) -> p t d", dict(d=DX))
        yo0, yo1 = parts(area_o, 4 * HC * 512 + 2 * PAIR, rows, rows)
        yo = [yo0, yo1]
        wkT, = parts(area_o, 0, (NH * LAT, None, None))
        wide = (2 * HID, "p (a n) -> p a n", dict(a=2))
        deep = (2 * HC * D, "p (a c n) -> p a c n", dict(a=2, c=HC))
        wgt0, wgt1, wut0, wut1, wdt0, wdt1, xe0, xe1 = parts(
            area_v, 0, wide, wide, wide, wide, deep, deep, xrows, xrows)
        wgt, wut, wdt, xe = [wgt0, wgt1], [wut0, wut1], [wdt0, wdt1], [xe0, xe1]
        oh, pc, geq = parts(yg[:].rearrange("p t k d -> p (t k d)"), 0, *[(HT * K * E, "p (n e) -> p n e", dict(e=E))] * 2,
                            (HT * KG * G, "p (n e) -> p n e", dict(e=G)))
        yT = parts(area_v, 0, (T, None, None), (T, None, None))

        s_const = sem("s_const")
        s_x = sem("s_x")
        s_cen = sem("s_cen")
        s_w = sem("s_w")
        s_zero = sem("s_zero")
        s_fill = sem("s_fill")
        s_filly = sem("s_filly")
        s_cst = sem("s_cst")
        s_dve = sem("s_dve")
        s_act = sem("s_act")
        s_cn = sem("s_cn")
        s_cnn = sem("s_cnn")
        s_ct = sem("s_ct")
        s_ctc = sem("s_ctc")
        s_wk = sem("s_wk")
        s_ax = sem("s_ax")
        ln_stat = sem("ln_stat")
        ln_std = sem("ln_std")
        xn_ready = sem("xn_ready")
        xnT_ps = sem("xnT_ps")
        xnT_ready = sem("xnT_ready")
        nrm_ready = sem("nrm_ready")
        sc_ready = sem("sc_ready")
        sc_read = sem("sc_read")
        sel_ready = sem("sel_ready")
        gd_ready = sem("gd_ready")
        ge_ready = sem("ge_ready")
        cum_ready = sem("cum_ready")
        slot_ready = sem("slot_ready")
        scat = sem("scat")
        sh_gu = sem("sh_gu")
        sh_sil = sem("sh_sil")
        sh_h = sem("sh_h")
        sh_y = sem("sh_y")
        sh_x = sem("sh_x")
        w_in = [sem(f"w_in{j}") for j in range(2)]
        x_in = [sem(f"x_in{j}") for j in range(2)]
        xeT_ps = sem("xeT_ps")
        xeT_sb = sem("xeT_sb")
        gu_ready = sem("gu_ready")
        sil_ready = sem("sil_ready")
        h_ready = sem("h_ready")
        y_ps = sem("y_ps")
        y_sb = sem("y_sb")
        idx_step = sem("idx_step")
        y_begun = sem("y_begun")
        y_out = [sem(f"y_out{j}") for j in range(2)]
        gath = [sem(f"gath{t}") for t in range(HT)]
        comb = sem("comb")
        v_ps = sem("v_ps")
        v_a = sem("v_a")
        v_d = sem("v_d")
        qk_ps = sem("qk_ps")
        tq_ready = sem("tq_ready")
        qk_split = sem("qk_split")
        kz_ready = sem("kz_ready")
        s_ready = sem("s_ready")
        smax = sem("smax")
        m_ready = sem("m_ready")
        mt_ready = sem("mt_ready")
        qc_ready = sem("qc_ready")
        st_ready = sem("st_ready")
        exp_done = sem("exp_done")
        pv_done = sem("pv_done")
        norm_done = sem("norm_done")
        yt_ps = sem("yt_ps")
        yt_a = sem("yt_a")
        yt_d = sem("yt_d")
        wo_ps = sem("wo_ps")
        wo_x = sem("wo_x")
        s_out = sem("s_out")

        ident = cst[:, C_ID:C_ID + P]
        block = ctx.enter_context(nc.Block())
        N_W = 13 * 16

        @block.sync
        def _(sp):
            sp.dma_start(cst[:], consts).then_inc(s_const, 16)
            for h in range(4):
                sp.dma_start(xs[:, 4 * h:4 * h + 4, :], x_t[:, 4 * h:4 * h + 4, :]).then_inc(s_x, 16)
            sp.dma_start(cen[0:G, :], gcen).then_inc(s_cen, 16)
            sp.dma_start(cen[G:G + E, :], ecen).then_inc(s_cen, 16)
            sp.dma_start(ebb[:], ebias.partition_broadcast(P)).then_inc(s_cen, 16)
            sp.wait_ge(s_zero, 3)
            zt = Kz[0][:].rearrange("p h t -> p (h t)").bitcast(F32)
            zrow = SLOTS * DX // P // 4
            xb_flat = xbuf.rearrange("(p c) d -> p (c d)", p=P)
            for k in range(4):
                sp.dma_start(xb_flat[:, k * zrow:(k + 1) * zrow], zt[:, 0:zrow]).then_inc(s_fill, 16)
            sp.dma_start(sgw[:], sg).then_inc(s_w, 16)
            sp.dma_start(suw[:], su).then_inc(s_w, 16)
            sp.dma_start(sdw[:], sd.rearrange("(c p) d -> p c d", p=P)).then_inc(s_w, 16)
            sp.dma_start(wkT, WkT).then_inc(s_w, 16)
            sp.dma_start(wq_in[:].rearrange("p h d -> p (h d)"), Wq).then_inc(s_w, 16)
            sp.dma_start(wv_in[:], Wv).then_inc(s_w, 16)
            sp.dma_start(wo_in[:], Wo.rearrange("(c p) d -> p c d", p=P)).then_inc(s_w, 16)
            for a in range(2):
                sp.dma_start(wcT[a * LAT:(a + 1) * LAT, a, :], WcT).then_inc(s_w, 16)
            sp.dma_start(bq2[:].rearrange("a h d -> a (h d)"), bq).then_inc(s_w, 16)
            sp.dma_start(bk2[:], bk).then_inc(s_w, 16)
            sp.dma_start(bvc[:], bv).then_inc(s_w, 16)
            sp.dma_start(bor[:], bo.rearrange("(a n) -> a n", a=1)).then_inc(s_w, 16)
            yb_flat = ybuf.rearrange("(p c) d -> p (c d)", p=P)
            for k in range(2):
                sp.dma_start(yb_flat[:, k * HG * T:(k + 1) * HG * T], zt).then_inc(s_filly, 16)

            def pair_in(L, n, j):
                if L or not isinstance(n, int) or n >= 2:
                    sp.wait_ge(y_sb, n * 2 + 2 * NPAIR * L)
                sp.dma_start(wgt[j], wg[bass.ds(n * 2, 2)].rearrange("e p h -> p e h")).then_inc(w_in[j], 16)
                sp.dma_start(wut[j], wu[bass.ds(n * 2, 2)].rearrange("e p h -> p e h")).then_inc(w_in[j], 16)
                for a in range(2):
                    sp.dma_start(wdt[j][:, a], wd[bass.ds(n * 2 + a, 1)].rearrange("e (c p) d -> p (e c) d", p=P))\
                        .then_inc(w_in[j], 16)
                sp.wait_ge(scat, 64 * 16 * (L + 1))
                sp.dma_start(xe[j], xbuf[bass.ds(n * PAIR, PAIR)].rearrange("(c p) d -> p c d", p=P)).then_inc(x_in[j], 16)

            def expert_pairs(L):
                for j in range(2):
                    pair_in(L, j, j)
                with sp.Fori(0, NPAIR // 2 - 1) as it:
                    for j in range(2):
                        pair_in(L, it * 2 + (j + 2), j)

            def results(L, H, t):
                if t == 0:
                    for j in range(2):
                        sp.wait_ge(y_out[j], 16 * PT * NPAIR // 2 * (L + 1))
                if 2 * L + H > 0:
                    sp.wait_ge(comb, (2 * L + H - 1) * HT + t + 1)
                tile = H * HT + t
                sp.dma_start(yg[:, t], ybuf[tile * P * K:(tile + 1) * P * K].rearrange("(p k) d -> p k d", k=K))\
                    .then_inc(gath[t], 16)

            expert_pairs(0)
            for t in range(HT):
                results(0, 0, t)
            for t in range(HT):
                results(0, 1, t)
            for Gi in range(B * NG):
                sp.wait_ge(qk_split, 2 * Gi + 2)
                sp.wait_ge(s_fill, 64)
                sp.wait_ge(s_filly, 32)
                for h in range(HG):
                    sp.dma_start(Kz[Gi % 2][RW * h:RW * h + RW, h, :].bitcast(F32),
                                 Kn[RW * h:RW * h + RW, :].bitcast(F32)).then_inc(kz_ready, 16)
            sp.wait_ge(wo_x, 2 * HT)
            expert_pairs(1)
            for t in range(HT):
                results(1, 0, t)
            for t in range(NT):
                if t < HT:
                    results(1, 1, t)
                sp.wait_ge(comb, NT + t + 1)
                sp.dma_start(out_t[:, t, :], xs[:, t, :]).then_inc(s_out, 16)
            sp.wait_ge(s_out, 16 * NT)

        @block.gpsimd
        def _(pool):
            for k in range(2):
                nc.gpsimd.memset(Kz[k][:].rearrange("p h t -> p (h t)").bitcast(F32), 0.0).then_inc(s_zero, 1)

            def scatter(L, H, lo, hi):
                pool.wait_ge(slot_ready, 2 * L + H + 1)
                pool.wait_ge(s_fill, 16 * 4)
                for t in range(lo, hi):
                    for k in range(K):
                        pool.indirect_dma_start(
                            xbuf[:, :], bass.IndirectOffsetOnAxis(ap=sidx[:, H, t * K + k:t * K + k + 1], axis=0),
                            xn[:, H * HT + t, :], None, bounds_check=SLOTS - 1, oob_is_err=False).then_inc(scat, 16)

            def results(L):
                pool.wait_ge(s_filly, 32)
                if L:
                    pool.wait_ge(comb, NT)
                with pool.Fori(0, NPAIR // 2) as it:
                    for j in range(2):
                        pool.wait_ge(y_sb, it * 4 + (2 * NPAIR * L + 2 * j + 4))
                        pool.sem_inc(y_begun, 1)
                        for t in range(PT):
                            pool.indirect_dma_start(
                                ybuf[:, :], bass.IndirectOffsetOnAxis(ap=yidx[:, j, t:t + 1], axis=0),
                                yo[j][:, t, :], None, bounds_check=RES - 1, oob_is_err=False).then_inc(y_out[j], 16)

            scatter(0, 0, 0, HT)
            scatter(0, 1, 0, HT)
            results(0)
            scatter(1, 0, 0, HT)
            scatter(1, 1, 0, HT)
            results(1)

        @block.scalar
        def _(act):
            act.wait_ge(s_const, 16)
            act.wait_ge(s_cen, 48)
            nc.scalar.activation(cenn[:], cen[:], ACT.Square, accum_out=csq[:, 0:1]).then_inc(s_act, 1)
            act.wait_ge(s_act, 1)
            nc.scalar.activation(csq[:, 1:2], csq[:, 0:1], ACT.Sqrt).then_inc(s_cn, 1)

            def ln_std_dev(r):
                act.wait_ge(ln_stat, r + 1)
                nc.scalar.activation(std[:], mv[:, :, 1], ACT.Sqrt, bias=cst[:, C_EPS:C_EPS + 1]).then_inc(ln_std, 1)

            def ln_scaled(r, H, norms):
                for q in range(2):
                    act.wait_ge(xnT_ps, 2 * r + q + 1)
                    nc.scalar.activation(xnT[:, H * T + 512 * q:H * T + 512 * q + 512], PS[:, q, :], ACT.Copy)\
                        .then_inc(xnT_ready, 1)
                if norms:
                    for t in range(HT):
                        act.wait_ge(xn_ready, HT * r + t + 1)
                        ins = nc.scalar.activation(sqj[:], xn[:, H * HT + t, 0:D], ACT.Square,
                                                   accum_out=ssq[:, t:t + 1])
                        ins.then_inc(s_act, 1)
                        n_act[0] += 1
                        act.wait_ge(s_act, n_act[0])
                    nc.scalar.activation(nrm[:, H, :], ssq[:], ACT.Sqrt).then_inc(nrm_ready, 1)

            n_act = [1]

            def gates(f):
                act.wait_ge(gd_ready, f + 1)
                nc.scalar.activation(ge[:, f % 2], gd[:, f % 2], ACT.Exp).then_inc(ge_ready, 1)

            def shared(L):
                for q in range(4):
                    for c in range(HC):
                        n = 8 * L + 2 * q + c
                        act.wait_ge(sh_gu, n + 1)
                        if n >= 4:
                            act.wait_ge(sh_h, n - 3)
                        nc.scalar.activation(sil[q % 2][:, c, :], PS[:, 2 + c, :], ACT.Silu).then_inc(sh_sil, 1)

            def experts(L):
                with act.Fori(0, NPAIR // 2) as it:
                    for j in range(2):
                        act.wait_ge(xeT_ps, it * 2 + (NPAIR * L + j + 1))
                        nc.scalar.activation(xeT[j][:], flat(0, 2)[:, 0:PAIR], ACT.Copy).then_inc(xeT_sb, 1)
                        for a in range(2):
                            for c in range(HC):
                                act.wait_ge(gu_ready, it * 8 + (4 * NPAIR * L + 4 * j + 2 * a + c + 1))
                                act.wait_ge(h_ready, it * 8 + (4 * NPAIR * L + 4 * j + 2 * a + c + 1))
                                nc.scalar.activation(sil[a][:, c, 0:CAP], PS[:, 2 + c, 0:CAP], ACT.Silu)\
                                    .then_inc(sil_ready, 1)

            def qk_round(Gi):
                for q, col in ((0, C_SQ), (1, C_SK)):
                    act.wait_ge(qk_ps, 2 * Gi + q + 1)
                    if Gi and q == 0:
                        act.wait_ge(qc_ready, Gi)
                    if Gi and q == 1:
                        act.wait_ge(kz_ready, 16 * HG * Gi)
                    nc.scalar.activation((Qn, Kn)[q][:], flat(2 * q, 2), ACT.Identity,
                                         scale=cst[:, col:col + 1]).then_inc(tq_ready, 1)

            def values(b):
                if b:
                    act.wait_ge(wo_ps, HT)
                for j in range(HT):
                    act.wait_ge(v_ps, HT * b + j + 1)
                    nc.scalar.activation(vs[:, j, 0:8, 0:LAT], PS[:, 2 * (j % 2), :].rearrange("p (h l) -> p h l", l=LAT),
                                         ACT.Copy).then_inc(v_a, 1)

            def heads(Gi):
                for n in range(SLOT):
                    N = SLOT * Gi + n
                    if n == AT_QK + 1 and Gi + 1 < B * NG:
                        qk_round(Gi + 1)
                    if n == AT_TR + 1 and Gi == G_LN1:
                        ln_scaled(3, 1, False)
                    if n == AT_TR + 1 and Gi == G_LN0:
                        ln_scaled(4, 0, True)
                    if n == AT_LN + 1 and Gi in (G_LN1, G_LN0):
                        ln_std_dev({G_LN1: 3, G_LN0: 4}[Gi])
                    if n == AT_S0 and Gi == G_ROUTE:
                        gates(2)
                    w = CHUNKS[n % NC][2]
                    act.wait_ge(st_ready, N + 1)
                    if N >= 4:
                        act.wait_ge(pv_done, N - 3)
                    nc.scalar.activation(pT[:, N % 4, 0:w], PS[:, 4 + N % 2, 0:w], ACT.Exp).then_inc(exp_done, 1)

            def out_rows(b):
                for i in range(HT):
                    n = HT * b + i
                    act.wait_ge(yt_ps, n + 1)
                    if n >= 2:
                        act.wait_ge(wo_ps, n - 1)
                    nc.scalar.activation(yT[i % 2][:, 0:512], PS[:, 2 * (i % 2), :], ACT.Copy).then_inc(yt_a, 1)

            for r, H, norms in ((0, 0, True), (1, 1, True)):
                ln_std_dev(r)
                ln_scaled(r, H, norms)
            gates(0)
            gates(1)
            shared(0)
            experts(0)
            ln_std_dev(2)
            ln_scaled(2, 0, False)
            for b in range(B):
                values(b)
                if b == 0:
                    qk_round(0)
                for g in range(NG):
                    heads(NG * b + g)
                out_rows(b)
            ln_std_dev(5)
            ln_scaled(5, 1, True)
            gates(3)
            shared(1)
            experts(1)

        @block.vector
        def _(dve):
            n_dve = [0]

            def link(ins):
                n_dve[0] += 1
                ins.then_inc(s_dve, 1)
                dve.wait_ge(s_dve, n_dve[0])

            tt, ts, stt = nc.vector.tensor_tensor, nc.vector.tensor_scalar, nc.vector.scalar_tensor_tensor
            nc.vector.memset(wcT[:], 0.0).then_inc(s_zero, 1)
            nc.vector.memset(M[:], 0.0)
            nc.vector.memset(mxp[:], -3.0e38)
            nc.vector.memset(wqx[:], 0.0)
            nc.vector.memset(wkx[:], 0.0)
            nc.vector.memset(bqf[:], 0.0)
            link(nc.vector.memset(bkf[:], 0.0))
            nc.vector.memset(bkf[:, :, 0:R0], 1.0)
            nc.vector.memset(ones2[:].bitcast(F32), 1.0)
            nc.vector.memset(xn[:, :, D:DX], 0.0)
            nc.vector.memset(st[:], 0.0)
            nc.vector.memset(mv[:], 0.0).then_inc(h_ready, 2)
            nc.vector.memset(rn[:], 0.0).then_inc(y_sb, 2)
            nc.vector.memset(rec[:], 0.0).then_inc(y_ps, 2)
            nc.vector.memset(gsum[:], 0.0)
            nc.vector.memset(mxm[:], 0.0)
            dve.wait_ge(s_const, 16)
            nc.vector.tensor_copy(identb[:], ident)
            nc.vector.tensor_copy(trib[:], cst[:, C_TRI:C_TRI + P])
            nc.vector.tensor_copy(onesb[:], cst[:, C_ONE:C_ONE + P])
            nc.vector.tensor_copy(causS[:], cst[:, C_CS:C_CS + P])
            link(nc.vector.tensor_copy(causT[:], cst[:, C_CT:C_CT + P]))
            nc.vector.memset(rstd[:], 0.0).then_inc(s_cst, 1)
            dve.wait_ge(s_cn, 1)
            link(ts(csq[:, 2:3], csq[:, 1:2], 1e-12, None, ALU.max))
            link(nc.vector.reciprocal(csq[:, 3:4], csq[:, 2:3]))
            ts(cenn[:], cen[:], csq[:, 3:4], None, ALU.mult).then_inc(s_cnn, 1)
            dve.wait_ge(s_ct, 1)
            nc.vector.tensor_copy(cenT[:], PS[:, 6, 0:G + E]).then_inc(s_ctc, 1)

            def fold():
                dve.wait_ge(s_w, N_W)
                dve.wait_ge(s_wk, 1)
                for r in range(3):
                    c = slice(R0 + HD * r, R0 + HD * r + HD)
                    ts(wqx[:, :, c], wq_in[:], SCALE, None, ALU.mult)
                    ts(bqf[:, :, c], bq2[:], SCALE, None, ALU.mult)
                    nc.vector.tensor_copy(wkx[:, :, c], PS[:, 6, 0:P].rearrange("p (h d) -> p h d", d=HD))
                    link(nc.vector.tensor_copy(bkf[:, :, c], PS[0:2, 7, 0:P].rearrange("p (h d) -> p h d", d=HD)))
                nc.vector.tensor_copy(brow[:], PS[0:1, 7, P:2 * P])
                for src, dst in ((bqf, bqx), (bkf, bkx)):
                    f = src[:].rearrange("p h r -> p (h r)")
                    link(ts(bqs[:].bitcast(F32R), f, cst[0:2, C_S2:C_S2 + 1], None, ALU.mult))
                    link(stt(dst[:], f, cst[0:2, C_L2:C_L2 + 1], bqs[:], ALU.mult, ALU.add))
                nc.vector.memset(rstd[:], 0.0).then_inc(s_ax, 1)

            def ln(r, H):
                t0 = H * HT
                for t in range(HT):
                    ins = nc.vector.bn_stats(st[:, t, :], xs[:, t0 + t, :])
                link(ins)
                for t in range(HT):
                    ins = nc.vector.bn_aggr(mv[:, t, :], st[:, t, :])
                ins.then_inc(ln_stat, 1)
                dve.wait_ge(ln_std, r + 1)
                link(nc.vector.reciprocal(rstd[:], std[:]))
                if r >= 2:
                    dve.wait_ge(scat, 64 * 16)
                for t in range(HT):
                    ts(xn[:, t0 + t, 0:D], xs[:, t0 + t, :], mv[:, t, 0:1], rstd[:, t:t + 1], ALU.subtract, ALU.mult)\
                        .then_inc(xn_ready, 1)

            def route_scores(f, H):
                bank = score_bank(f)
                dve.wait_ge(nrm_ready, f + 1)
                link(ts(rn[:], nrm[:, H, :], 1e-12, None, ALU.max))
                link(nc.vector.reciprocal(rn[:], rn[:]))
                dve.wait_ge(sc_ready, f + 1)
                sc = PS[:, bank, 0:HT * (G + E)].rearrange("p (t n) -> p t n", n=G + E)
                link(tt(gs[:], sc[:, :, 0:G], rn[:].unsqueeze(2).broadcast_to([P, HT, G]), ALU.mult))
                tt(es[:], sc[:, :, G:G + E], rn[:].unsqueeze(2).broadcast_to([P, HT, E]), ALU.mult).then_inc(sc_read, 1)

            def route_choice(f, H):
                dve.wait_ge(sc_read, f + 1)
                link(tt(es[:], es[:], ebb[:].unsqueeze(1).broadcast_to([P, HT, E]), ALU.add))
                for t in range(HT):
                    ins = nc.vector.max(v8[:, t, :], gs[:, t, :])
                link(ins)
                for t in range(HT):
                    ins = nc.vector.max_index(i8[:, t, :], v8[:, t, :], gs[:, t, :])
                link(ins)
                link(nc.vector.tensor_copy(idf[:], i8[:, :, 0:KG]))
                link(tt(geq[:], cst[:, C_I8:C_I8 + G].unsqueeze(1).broadcast_to([P, HT * KG, G]),
                        idf[:].rearrange("p t k -> p (t k)").unsqueeze(2).broadcast_to([P, HT * KG, G]), ALU.is_equal))
                link(nc.vector.tensor_reduce(gm[:], geq[:].rearrange("p (t k) g -> p t g k", k=KG), AX.X, ALU.add))
                ts(pen[:], gm[:], 1.0e9, -1.0e9, ALU.mult, ALU.add)
                gmf = gm[:].rearrange("p t g -> p (t g)").unsqueeze(2).broadcast_to([P, HT * G, EG])
                pnf = pen[:].rearrange("p t g -> p (t g)").unsqueeze(2).broadcast_to([P, HT * G, EG])
                mkf = mk[:].rearrange("p t (g e) -> p (t g) e", e=EG)
                link(tt(mkf, es[:].rearrange("p t (g e) -> p (t g) e", e=EG), gmf, ALU.mult))
                link(tt(mkf, mkf, pnf, ALU.add))
                for t in range(HT):
                    ins = nc.vector.max(v8[:, t, :], mk[:, t, :])
                link(ins)
                tt(gd[:, H], v8[:, :, 0:K], v8[:, :, 0:1].broadcast_to([P, HT, K]), ALU.subtract).then_inc(gd_ready, 1)
                for t in range(HT):
                    ins = nc.vector.max_index(i8[:, t, :], v8[:, t, :], mk[:, t, :])
                link(ins)
                link(nc.vector.tensor_copy(eif[:], i8[:, :, 0:K]))
                link(tt(oh[:], cst[:, C_I32:C_I32 + E].unsqueeze(1).broadcast_to([P, HT * K, E]),
                        eif[:].rearrange("p t k -> p (t k)").unsqueeze(2).broadcast_to([P, HT * K, E]), ALU.is_equal))
                with nc.allow_low_precision("zeros and ones"):
                    nc.vector.tensor_reduce(sel[:, H * HT:H * HT + HT, :], oh[:].rearrange("p (t k) e -> p t e k", k=K),
                                            AX.X, ALU.add).then_inc(sel_ready, 1)

            def route_slots(f, H):
                dve.wait_ge(ge_ready, f + 1)
                link(nc.vector.tensor_reduce(gsum[:], ge[:, H], AX.X, ALU.add))
                link(nc.vector.reciprocal(gsum[:], gsum[:]))
                tt(ge[:, H], ge[:, H], gsum[:].unsqueeze(2).broadcast_to([P, HT, K]), ALU.mult)
                dve.wait_ge(cum_ready, f + 1)
                cnt = PS[:, score_bank(f) + 1, H * HT * E:(H + 1) * HT * E].rearrange("p (t e) -> p t e", e=E)
                link(tt(pc[:].rearrange("p (t k) e -> p t k e", k=K), oh[:].rearrange("p (t k) e -> p t k e", k=K),
                        cnt.unsqueeze(2).broadcast_to([P, HT, K, E]), ALU.mult))
                link(nc.vector.tensor_reduce(pos[:], pc[:], AX.X, ALU.add))
                ts(over[:], pos[:], float(CAP), float(SKIP), ALU.is_gt, ALU.mult)
                ts(keep[:], pos[:], float(CAP), 0.5, ALU.is_le, ALU.mult)
                link(stt(slf[:], eif[:].rearrange("p t k -> p (t k)"), float(CAP), pos[:], ALU.mult, ALU.add))
                nc.vector.tensor_copy(xn[:, H * HT:H * HT + HT, X_EXP:X_EXP + K], eif[:])
                ts(xn[:, H * HT:H * HT + HT, X_TOK], cst[:, C_TOK + H * HT:C_TOK + H * HT + HT],
                   float(LAYER * (f // 2)), None, ALU.add)
                link(tt(gate[:, H, :], ge[:, H].rearrange("p t k -> p (t k)"), keep[:], ALU.mult))
                stt(sidx[:, H, :], slf[:], -1.0, over[:], ALU.add, ALU.add).then_inc(slot_ready, 1)

            def shared(L):
                for q in range(4):
                    for c in range(HC):
                        n = 8 * L + 2 * q + c
                        dve.wait_ge(sh_sil, n + 1)
                        if n >= 4:
                            dve.wait_ge(sh_y, (n - 4) // 2 + 1)
                        tt(hb[q % 2][:, c, :], sil[q % 2][:, c, :], PS[:, 4 + c, :], ALU.mult).then_inc(sh_h, 1)
                    if q:
                        shared_x(L, q - 1)
                shared_x(L, 3)

            def shared_x(L, q):
                dve.wait_ge(sh_y, 4 * L + q + 1)
                xq = xs[:, 4 * q:4 * q + 4, :].rearrange("p t d -> p (t d)")
                stt(xq, PS[:, 6 + q % 2, :], 0.5, xq, ALU.mult, ALU.add).then_inc(sh_x, 1)

            def result_rows(L, it, j):
                def step(i):
                    return it * 8 + (4 * NPAIR * L + 4 * j + i)
                dve.wait_ge(x_in[j], it * 16 + (16 * NPAIR // 2 * L + 16))
                tt(hit[:], xe[j][:, :, X_EXP:X_EXP + K], eid[:].unsqueeze(2).broadcast_to([P, PT, K]), ALU.is_equal)\
                    .then_inc(idx_step, 1)
                dve.wait_ge(idx_step, step(1))
                ts(eid[:], eid[:], 2.0, None, ALU.add)
                tt(hit[:], hit[:], cst[:, C_K:C_K + K].unsqueeze(1).broadcast_to([P, PT, K]), ALU.mult).then_inc(idx_step, 1)
                dve.wait_ge(idx_step, step(2))
                nc.vector.tensor_reduce(kth[:], hit[:], AX.X, ALU.add).then_inc(idx_step, 1)
                dve.wait_ge(idx_step, step(3))
                if L or not isinstance(it, int) or it:
                    dve.wait_ge(y_out[j], it * (16 * PT) + 16 * PT * NPAIR // 2 * L)
                stt(yidx[:, j, :], kth[:], float(LAYER * (L + 1)), xe[j][:, :, X_TOK], ALU.add, ALU.subtract)\
                    .then_inc(idx_step, 1)
                dve.wait_ge(idx_step, step(4))

            def experts(L):
                link(nc.vector.tensor_copy(eid[:], cst[:, C_EID:C_EID + PT]))
                two_pairs(L, 0)
                with dve.Fori(0, NPAIR // 2 - 1) as it:
                    two_pairs(L, it + 1)

            def two_pairs(L, it):
                for j in range(2):
                    for a in range(2):
                        for c in range(HC):
                            dve.wait_ge(sil_ready, it * 8 + (4 * NPAIR * L + 4 * j + 2 * a + c + 1))
                            if c == 0:
                                dve.wait_ge(y_ps, it * 4 + (2 * NPAIR * L + 2 * j + a) + 1)
                            tt(hb[a][:, c, 0:CAP], sil[a][:, c, 0:CAP], PS[:, 4 + c, 0:CAP], ALU.mult)\
                                .then_inc(h_ready, 1)
                    result_rows(L, it, j)
                    for a in range(2):
                        dve.wait_ge(y_ps, it * 4 + (2 * NPAIR * L + 2 * j + a + 3))
                        ya = PS[:, 6 + a, 0:3 * D].rearrange("p (t d) -> p t d", d=D)
                        if a == 0:
                            nc.vector.tensor_copy(yo[j][:, 0:2, :], ya[:, 0:2, :])
                            nc.vector.tensor_copy(yo[j][0:64, 2, :], ya[0:64, 2, :]).then_inc(y_sb, 1)
                        else:
                            nc.vector.tensor_copy(yo[j][64:P, 2, :], ya[64:P, 0, :])
                            nc.vector.tensor_copy(yo[j][:, 3:5, :], ya[:, 1:3, :]).then_inc(y_sb, 1)

            def combine(L, H):
                for t in range(HT):
                    dve.wait_ge(gath[t], 16 * (2 * L + H + 1))
                    xt = xs[:, H * HT + t, :]
                    for k in range(K):
                        ins = stt(xt, yg[:, t, k, :], gate[:, H, t * K + k:t * K + k + 1], xt, ALU.mult, ALU.add)
                        if k < K - 1:
                            link(ins)
                    ins.then_inc(comb, 1)
                dve.wait_ge(comb, HT * (2 * L + H + 1))

            def qk_parts(Gi):
                for q, (dst, col) in enumerate(((Qn, C_LQ), (Kn, C_LK))):
                    dve.wait_ge(tq_ready, 2 * Gi + q + 1)
                    stt(dst[:], flat(2 * q, 2), cst[:, col:col + 1], dst[:].bitcast(F32), ALU.mult, ALU.add)\
                        .then_inc(qk_split, 1)

            def row_max(Gi, s):
                i, c, w = ROWS[s // 2]
                hp = s % 2
                dve.wait_ge(s_ready, NS * Gi + s + 1)
                nc.vector.tensor_reduce(mxp[:, i, c, 2 * hp:2 * hp + 2], PS[:, 2 * hp:2 * hp + 2, 0:w], AX.X, ALU.max)\
                    .then_inc(smax, 1)

            def max_parts(Gi):
                dve.wait_ge(smax, NS * Gi + NS)
                link(tt(mxm[:], mxp[:, :, 0, :], mxp[:, :, 1, :], ALU.max))
                if Gi:
                    dve.wait_ge(mt_ready, Gi)
                link(ts(M[:, :, :, 0].bitcast(F32R), mxm[:], -1.0, None, ALU.mult))
                stt(M[:, :, :, 1].bitcast(F32R), mxm[:], -1.0, M[:, :, :, 0], ALU.mult, ALU.subtract)\
                    .then_inc(m_ready, 1)

            def q_with_max(Gi):
                dve.wait_ge(mt_ready, Gi + 1)
                tt(Qc[Gi % 2][:], flat(0, 2), Qn[:].bitcast(F32), ALU.add).then_inc(qc_ready, 1)

            def normalise(Gi, hh, half):
                X = HG * Gi + hh
                dve.wait_ge(pv_done, SLOT * Gi + NC * hh + (4 if half == 0 else NC))
                o = PS[:, 6 + half, :].rearrange("p (t l) -> p t l", l=P)
                link(nc.vector.reciprocal(rec[:, half], o[:, :, LAT:VW]))
                h = (Gi % NG) * HG + hh
                tt(os_[:, 4 * half:4 * half + 4, h * LAT:(h + 1) * LAT], o[:, :, 0:LAT],
                   rec[:, half].broadcast_to([P, 4, LAT]), ALU.mult).then_inc(norm_done, 1)

            def values(b):
                if b:
                    dve.wait_ge(wo_ps, HT)
                nc.vector.memset(area_v[:, HT * NH * VW:], 0.0)
                nc.vector.memset(vs[:, :, :, LAT:VW], 1.0)
                for j in range(HT):
                    dve.wait_ge(v_ps, HT * b + j + 1)
                    nc.vector.tensor_copy(vs[:, j, 8:16, 0:LAT],
                                          PS[:, 2 * (j % 2) + 1, :].rearrange("p (h l) -> p h l", l=LAT)).then_inc(v_d, 1)

            def heads(Gi):
                for n in range(SLOT):
                    if n % NC == 6:
                        normalise(Gi, n // NC, 0)
                    if n % NC == 2 and n > NC:
                        normalise(Gi, n // NC - 1, 1)
                    if Gi + 1 < B * NG:
                        if n == AT_SPLIT:
                            qk_parts(Gi + 1)
                        if AT_S0 <= n < AT_MAX:
                            row_max(Gi + 1, n - AT_S0)
                        if n == AT_MAX:
                            max_parts(Gi + 1)
                        if n == AT_QC:
                            q_with_max(Gi + 1)
                    if n == AT_LN:
                        if Gi == G_COMB:
                            combine(0, 1)
                        if Gi == G_LN1:
                            ln(3, 1)
                        if Gi == G_LN0:
                            ln(4, 0)
                        if Gi == G_ROUTE:
                            route_choice(2, 0)
                    if n == AT_READ and Gi == G_LN0:
                        route_scores(2, 0)
                    if n == AT_READ and Gi == G_ROUTE:
                        route_slots(2, 0)
                normalise(Gi, HG - 1, 1)

            def out_rows(b):
                for i in range(HT):
                    n = HT * b + i
                    dve.wait_ge(yt_ps, n + 1)
                    if n >= 2:
                        dve.wait_ge(wo_ps, n - 1)
                    nc.vector.tensor_copy(yT[i % 2][:, 512:1024], PS[:, 2 * (i % 2) + 1, :]).then_inc(yt_d, 1)
                    if i:
                        add_x(b, i - 1)
                add_x(b, HT - 1)
                dve.wait_ge(wo_x, HT * (b + 1))

            def add_x(b, i):
                dve.wait_ge(wo_ps, HT * b + i + 1)
                xt = xs[:, HT * b + i, :]
                tt(xt, PS[:, 6 + i % 2, 0:D], xt, ALU.add).then_inc(wo_x, 1)

            dve.wait_ge(s_x, 64)
            ln(0, 0)
            ln(1, 1)
            for f in range(2):
                for step in (route_scores, route_choice, route_slots):
                    step(f, f)
            fold()
            shared(0)
            experts(0)
            combine(0, 0)
            ln(2, 0)
            for b in range(B):
                values(b)
                if b == 0:
                    qk_parts(0)
                    for s in range(NS):
                        row_max(0, s)
                    max_parts(0)
                    q_with_max(0)
                for g in range(NG):
                    heads(NG * b + g)
                out_rows(b)
            ln(5, 1)
            for step in (route_scores, route_choice, route_slots):
                step(3, 1)
            shared(1)
            experts(1)
            combine(1, 0)
            combine(1, 1)

        @block.tensor
        def _(pe):
            mm = nc.tensor.matmul

            def ln(r, H):
                for q in range(2):
                    for t in range(4):
                        tile = 4 * q + t
                        pe.wait_ge(xn_ready, HT * r + tile + 1)
                        ins = nc.tensor.transpose(PS[:, q, t * P:(t + 1) * P], xn[:, H * HT + tile, 0:D], ident)
                    ins.then_inc(xnT_ps, 1)

            def scores(f, r, H):
                pe.wait_ge(xnT_ready, 2 * r + 2)
                for t in range(HT):
                    c0 = (H * HT + t) * P
                    ins = mm(PS[:, score_bank(f), t * (G + E):(t + 1) * (G + E)], xnT[:, c0:c0 + P], cenT[:], start=True, stop=True)
                ins.then_inc(sc_ready, 1)

            def counts(f, H):
                pe.wait_ge(sel_ready, f + 1)
                t0, t1 = H * HT, H * HT + HT
                def cols(a, b):
                    return PS[:, score_bank(f) + 1, a * E:b * E]
                for j in range(t1 - 1):
                    a = max(j + 1, t0)
                    mm(cols(a, t1).rearrange("p (t e) -> p t e", e=E), onesb[:],
                       sel[:, j:j + 1, :].broadcast_to([P, t1 - a, E]), start=(j == 0), stop=False, skip_group_check=True)
                mm(cols(t0, t1), trib[:], sel[:, t0:t1, :].rearrange("p t e -> p (t e)"), start=False, stop=True,
                   skip_group_check=True).then_inc(cum_ready, 1)

            def shared(L):
                def down(q):
                    pe.wait_ge(sh_h, 8 * L + 2 * q + 2)
                    if q >= 2:
                        pe.wait_ge(sh_x, 4 * L + q - 1)
                    for c in range(HC):
                        for t in range(4):
                            ins = mm(PS[:, 6 + q % 2, t * D:(t + 1) * D], hb[q % 2][:, c, t * P:(t + 1) * P], sdw[:, c, :],
                                     start=(c == 0 and t == 0), stop=(c == HC - 1), skip_group_check=True)
                    ins.then_inc(sh_y, 1)

                for q in range(4):
                    for c in range(HC):
                        n = 8 * L + 2 * q + c
                        if q:
                            pe.wait_ge(sh_h, n - 1)
                        rhs = xnT[:, 512 * q:512 * q + 512]
                        mm(PS[:, 2 + c, :], sgw[:, c * P:(c + 1) * P], rhs, start=True, stop=True)
                        mm(PS[:, 4 + c, :], suw[:, c * P:(c + 1) * P], rhs, start=True, stop=True).then_inc(sh_gu, 1)
                    if q:
                        down(q - 1)
                down(3)

            def experts(L):
                pe.wait_ge(sh_x, 4 * L + 4)
                with pe.Fori(0, NPAIR // 2) as it:
                    for j in range(2):
                        pe.wait_ge(x_in[j], it * 16 + (16 * NPAIR // 2 * L + 16))
                        for t in range(PT):
                            ins = nc.tensor.transpose(flat(0, 2)[:, t * P:(t + 1) * P], xe[j][:, t, 0:D], ident)
                        ins.then_inc(xeT_ps, 1)
                        pe.wait_ge(w_in[j], it * 64 + (64 * NPAIR // 2 * L + 64))
                        pe.wait_ge(xeT_sb, it * 2 + (NPAIR * L + j + 1))
                        for a in range(2):
                            gate_up(L, it, j, a)
                            if a:
                                down(L, it, j, 0)
                        down(L, it, j, 1)

            def gate_up(L, it, j, a):
                rhs = xeT[j][:, a * CAP:(a + 1) * CAP]
                for c in range(HC):
                    pe.wait_ge(h_ready, it * 8 + (4 * NPAIR * L + 4 * j + 2 * a + c + 1))
                    mm(PS[:, 2 + c, 0:CAP], wgt[j][:, a, c * P:(c + 1) * P], rhs, start=True, stop=True)
                    mm(PS[:, 4 + c, 0:CAP], wut[j][:, a, c * P:(c + 1) * P], rhs, start=True, stop=True)\
                        .then_inc(gu_ready, 1)

            def down(L, it, j, a):
                pe.wait_ge(y_sb, it * 4 + (2 * NPAIR * L + 2 * j + a + 1))
                tiles = ((0, P, 0, 0), (P, P, 0, 1), (2 * P, 64, 0, 2)) if a == 0 else \
                    ((64, P, 0, 1), (64 + P, P, 0, 2), (0, 64, 64, 0))
                for c in range(HC):
                    pe.wait_ge(h_ready, it * 8 + (4 * NPAIR * L + 4 * j + 2 * a + c + 3))
                    for n, (col, m, p0, t) in enumerate(tiles):
                        ins = mm(PS[p0:p0 + m, 6 + a, t * D:(t + 1) * D], hb[a][:, c, col:col + m], wdt[j][:, a, c, :],
                                 start=(c == 0 and n == 0) , stop=(c == HC - 1), skip_group_check=True)
                ins.then_inc(y_ps, 1)

            def values(b):
                for j in range(HT):
                    if j >= 2:
                        pe.wait_ge(v_a, HT * b + j - 1)
                        pe.wait_ge(v_d, HT * b + j - 1)
                    for c in range(2):
                        ins = mm(PS[:, 2 * (j % 2) + c, :], xnT[:, (HT * b + j) * P:(HT * b + j + 1) * P],
                                 wv_in[:, 512 * c:512 * c + 512], start=True, stop=True)
                    ins.then_inc(v_ps, 1)
                pe.wait_ge(v_a, HT * (b + 1))
                pe.wait_ge(v_d, HT * (b + 1))

            def qk(Gi):
                b, g = Gi // NG, Gi % NG
                if Gi:
                    pe.wait_ge(qc_ready, Gi)
                if Gi == G_LN1 + 2:
                    pe.wait_ge(xnT_ready, 8)
                gc = slice(g * HG * RW, (g + 1) * HG * RW)
                for q, (w, bias) in enumerate(((wqx, bqx), (wkx, bkx))):
                    for c in range(2):
                        o = PS[:, 2 * q + c, :]
                        mm(o, w[:].rearrange("p h r -> p (h r)")[:, gc], xnT[:, b * T + 512 * c:b * T + 512 * c + 512],
                           start=True, stop=False)
                        ins = mm(o, bias[:, gc], ones2[:], start=False, stop=True)
                    ins.then_inc(qk_ps, 1)

            def s_rows(Gi, s):
                i, c, w = ROWS[s // 2]
                hp = s % 2
                if s == 0:
                    if Gi == G_LN1 + 1:
                        pe.wait_ge(xnT_ready, 8)
                    if Gi == G_LN0 + 1:
                        pe.wait_ge(sc_read, 3)
                    if Gi == G_ROUTE + 1:
                        pe.wait_ge(slot_ready, 3)
                    pe.wait_ge(qk_split, 2 * Gi + 2)
                    pe.wait_ge(kz_ready, 16 * HG * (Gi + 1))
                if s >= 2:
                    pe.wait_ge(smax, NS * Gi + s - 1)
                diag = c == i // 4
                for hh in range(2):
                    o = PS[:, 2 * hp + hh, 0:w]
                    ins = mm(o, Qn[:, i * P:(i + 1) * P], Kz[Gi % 2][:, 2 * hp + hh, 512 * c:512 * c + w],
                             start=True, stop=not diag)
                    if diag:
                        ins = mm(o[:, w - P:w], identb[:], causS[:], start=False, stop=True)
                ins.then_inc(s_ready, 1)

            def max_rows(Gi):
                pe.wait_ge(m_ready, Gi + 1)
                for i in range(HT):
                    ins = nc.tensor.transpose(flat(0, 2)[:, i * P:(i + 1) * P], M[:, i].rearrange("p h r -> p (h r)"), ident)
                ins.then_inc(mt_ready, 1)

            def s_cols(Gi, n):
                N = SLOT * Gi + n
                j, t0, w, _ = CHUNKS[n % NC]
                if N >= 2:
                    pe.wait_ge(exp_done, N - 1)
                diag = t0 == j * P
                o = PS[:, 4 + N % 2, 0:w]
                ins = mm(o, Kz[Gi % 2][:, n // NC, j * P:(j + 1) * P], Qc[Gi % 2][:, t0:t0 + w], start=True, stop=not diag)
                if diag:
                    ins = mm(o[:, 0:P], identb[:], causT[:], start=False, stop=True)
                ins.then_inc(st_ready, 1)

            def pv(Gi, n):
                N = SLOT * Gi + n
                j, t0, w, half = CHUNKS[n % NC]
                X = HG * Gi + n // NC
                first = n % NC == (0 if half == 0 else 4)
                if first and X:
                    pe.wait_ge(norm_done, 2 * X - 1 + half)
                pe.wait_ge(exp_done, N + 1)
                h = (Gi % NG) * HG + n // NC
                for k in range(w // P):
                    i = t0 // P + k
                    ins = mm(PS[:, 6 + half, (i % 4) * P:(i % 4 + 1) * P], pT[:, N % 4, k * P:(k + 1) * P],
                             area_v[:, (j * NH + h) * VW:(j * NH + h) * VW + P],
                             start=(first and k == 0), stop=(i == j), skip_group_check=True)
                ins.then_inc(pv_done, 1)

            def heads(Gi):
                pe.wait_ge(qc_ready, Gi + 1)
                for n in range(SLOT):
                    s_cols(Gi, n)
                    if n >= 2:
                        pv(Gi, n - 2)
                    if Gi + 1 < B * NG:
                        if n == AT_QK:
                            qk(Gi + 1)
                        if AT_S0 <= n < AT_MAX:
                            s_rows(Gi + 1, n - AT_S0)
                        if n == AT_MT:
                            max_rows(Gi + 1)
                    if n == AT_TR and Gi in (G_LN1, G_LN0):
                        pe.wait_ge(qk_split, 2 * Gi + 4)
                        ln(*{G_LN1: (3, 1), G_LN0: (4, 0)}[Gi])
                    if n == AT_SC and Gi == G_LN0:
                        scores(2, 4, 0)
                    if n == AT_CNT and Gi == G_ROUTE:
                        pe.wait_ge(qk_split, 2 * Gi + 4)
                        counts(2, 0)
                pv(Gi, SLOT - 2)
                pv(Gi, SLOT - 1)

            def out_rows(b):
                pe.wait_ge(norm_done, 2 * NH * (b + 1))
                for i in range(HT):
                    n = HT * b + i
                    if i >= 2:
                        pe.wait_ge(yt_a, n - 1)
                        pe.wait_ge(yt_d, n - 1)
                    for c in range(8):
                        ins = nc.tensor.transpose(flat(2 * (i % 2), 2)[:, c * P:(c + 1) * P], os_[:, i, c * P:(c + 1) * P], ident)
                    ins.then_inc(yt_ps, 1)
                    if i:
                        out_proj(b, i - 1)
                out_proj(b, HT - 1)
                pe.wait_ge(wo_x, HT * (b + 1))

            def out_proj(b, i):
                n = HT * b + i
                pe.wait_ge(yt_a, n + 1)
                pe.wait_ge(yt_d, n + 1)
                if i >= 2:
                    pe.wait_ge(wo_x, n - 1)
                o = PS[:, 6 + i % 2, 0:D]
                mm(o, cst[0:1, C_ONE:C_ONE + P], brow[:], start=True, stop=False)
                for c in range(8):
                    ins = mm(o, yT[i % 2][:, c * P:(c + 1) * P], wo_in[:, c, :], start=False, stop=(c == 7))
                ins.then_inc(wo_ps, 1)

            pe.wait_ge(s_const, 16)
            pe.wait_ge(s_cst, 1)
            pe.wait_ge(s_cnn, 1)
            nc.tensor.transpose(PS[:, 6, 0:G + E], cenn[:], ident[0:G + E, 0:G + E]).then_inc(s_ct, 1)
            pe.wait_ge(s_w, N_W)
            pe.wait_ge(s_ctc, 1)
            ln(0, 0)
            scores(0, 0, 0)
            ln(1, 1)
            pe.wait_ge(sc_read, 1)
            scores(1, 1, 1)
            counts(0, 0)
            counts(1, 1)
            pe.wait_ge(slot_ready, 2)
            wc2 = wcT[:].rearrange("p a d -> p (a d)")
            for c in range(8):
                mm(PS[:, 6, c * 2 * HD:(c + 1) * 2 * HD], wkT[:, c * P:(c + 1) * P], wc2, start=True, stop=True)
                mm(PS[0:2, 7, c * 2 * HD:(c + 1) * 2 * HD], bk2[:, c, :], wc2, start=True, stop=True)
            mm(PS[0:1, 7, P:2 * P], cst[0:1, C_ONE:C_ONE + 1], bor[:], start=True, stop=False)
            for c in range(8):
                ins = mm(PS[0:1, 7, P:2 * P], bvc[:, c:c + 1], wo_in[:, c, :], start=False, stop=(c == 7))
            ins.then_inc(s_wk, 1)
            pe.wait_ge(s_ax, 1)
            shared(0)
            experts(0)
            ln(2, 0)
            pe.wait_ge(xnT_ready, 6)
            for b in range(B):
                values(b)
                if b == 0:
                    qk(0)
                    for s in range(NS):
                        s_rows(0, s)
                    max_rows(0)
                for g in range(NG):
                    heads(NG * b + g)
                out_rows(b)
            ln(5, 1)
            scores(3, 5, 1)
            counts(3, 1)
            pe.wait_ge(slot_ready, 4)
            shared(1)
            experts(1)


_INS = ['L0_attn_x', 'L0_attn_Wq', 'L0_attn_bq', 'L0_attn_Wk', 'L0_attn_bk', 'L0_attn_Wv', 'L0_attn_bv', 'L0_attn_Wo',
        'L0_attn_bo', 'L0_attn_Wc', 'L0_ffn_group_centroids', 'L0_ffn_expert_centroids', 'L0_ffn_bias', 'L0_ffn_wg',
        'L0_ffn_wu', 'L0_ffn_wd', 'L0_ffn_sg', 'L0_ffn_su', 'L0_ffn_sd']


def shape_constants():
    import numpy as np
    c = np.zeros((P, C_N), np.float32)
    p, q = np.arange(P)[:, None], np.arange(P)[None, :]
    c[:, C_ID:C_ID + P] = p == q
    c[:, C_TRI:C_TRI + P] = p <= q
    c[:, C_CS:C_CS + P] = np.where(q > p, NEG, 0.0)
    c[:, C_CT:C_CT + P] = np.where(p > q, NEG, 0.0)
    c[:, C_I8:C_I8 + G] = np.arange(G)
    c[:, C_I32:C_I32 + E] = np.arange(E)
    r = np.arange(P) % RW
    lo_q = (r >= R0 + 2 * HD) & (r < R0 + 3 * HD)
    lo_k = (r >= R0 + HD) & (r < R0 + 2 * HD)
    lo_2 = np.arange(P) == 1
    for lo, s, l in ((lo_q, C_SQ, C_LQ), (lo_k, C_SK, C_LK), (lo_2, C_S2, C_L2)):
        c[:, s] = np.where(lo, -1.0, 1.0)
        c[:, l] = lo
    c[:, C_TOK:C_TOK + NT] = LAYER - K * (q[:, 0:NT] * P + p)
    c[:, C_EID:C_EID + PT] = (q[:, 0:PT] * P + p) // CAP
    c[:, C_K:C_K + K] = np.arange(K)
    c[:, C_EPS] = 1e-5
    c[:, C_ONE:C_ONE + P] = 1.0
    return c


def layouts(inputs):
    import numpy as np
    a = {n: np.asarray(inputs[n]) for n in _INS[1:10]}
    pairs = NH * LAT // P
    return {
        'L0_attn_bq': np.stack([a['L0_attn_bq']] * 2),
        'L0_attn_Wk': a['L0_attn_Wk'].T.reshape(pairs, P, D).transpose(1, 0, 2).reshape(P, -1),
        'L0_attn_bk': np.stack([a['L0_attn_bk'].reshape(pairs, P).T] * 2, axis=2),
        'L0_attn_bv': a['L0_attn_bv'].reshape(pairs, P).T,
        'L0_attn_Wc': a['L0_attn_Wc'].T,
    }


def kernel(**inputs):
    import numpy as _np
    import concourse.bacc as _bacc
    from concourse import mybir as _mybir
    from concourse.bass_utils import run_bass_kernel_spmd as _run

    nc = _bacc.Bacc("TRN2", target_bir_lowering=False, num_devices=1)
    arrays, args = {}, []
    laid = layouts(inputs)
    for name in _INS:
        a = _np.ascontiguousarray(laid.get(name, inputs[name]))
        arrays[f"in_{name}_dram"] = a
        args.append(nc.dram_tensor(f"in_{name}_dram", a.shape, _mybir.dt.from_np(a.dtype), kind="ExternalInput").ap())
    arrays["in_consts_dram"] = shape_constants()
    args.append(nc.dram_tensor("in_consts_dram", (P, C_N), _mybir.dt.float32, kind="ExternalInput").ap())
    args.append(nc.dram_tensor("out_0_dram", (B, T, D), _mybir.dt.float32, kind="ExternalOutput").ap())
    program(nc, *args)
    r = _run(nc, [arrays], core_ids=[0])
    return r.results[0]["out_0_dram"]
```

```python
from contextlib import ExitStack

import concourse.bass as bass
from concourse import mybir

F32 = mybir.dt.float32
F32R = mybir.dt.float32r
BF16 = mybir.dt.bfloat16
U32 = mybir.dt.uint32
I32 = mybir.dt.int32
ALU = mybir.AluOpType
ACT = mybir.ActivationFunctionType
AX = mybir.AxisListType

P = 128
B, T, D = 2, 1024, 128
NT = B * T // P
HT = T // P
E, G, K = 32, 8, 4
EG = E // G
KG = G // 2
HID = 256
HC = HID // P
CAP = int(B * T / E * K * 1.25)
PAIR = 2 * CAP
PT = PAIR // P
NPAIR = E // 2
SLOTS = E * CAP
SKIP = 2 * SLOTS
DX = D + 8
X_TOK, X_EXP = D, D + 1
RES = K * B * T
LAYER = 2 * RES
NH, LAT, HD = 16, 64, 8
HG = 4
NG = NH // HG
RW = 32
R0 = 2
VW = LAT + 1
SCALE = 1.0 / 8.0
NEG = -1.0e30

C_ID, C_TRI, C_CS, C_ONE, C_I8, C_I32 = 0, 128, 256, 384, 512, 520
C_SQ, C_LQ, C_SK, C_LK, C_S2, C_L2, C_EPS = 552, 553, 554, 555, 556, 557, 558
C_TOK, C_EID, C_K, C_N = 560, 576, 581, 585

ROWS = [(i, c, min(512, (i + 1) * P) if c == 0 else (i - 3) * P) for i in range(HT) for c in range(1 + i // 4)]
NS = 2 * len(ROWS)
CHUNKS = [(j, j * P, 512 - j * P, 0) for j in range(4)] + \
         [(j, max(512, j * P), 1024 - max(512, j * P), 1) for j in range(8)]
NC = len(CHUNKS)
SLOT = HG * NC
LAG = 3
DIAG = [n for n, (j, t0, w, _) in enumerate(CHUNKS) if t0 == j * P]


AT_QK, AT_SPLIT, AT_COMB, AT_TR, AT_CNT, AT_SLOTS, AT_S0 = 0, 2, 3, 11, 7, 9, 18
AT_MAX, AT_MT, AT_QC = AT_S0 + NS, AT_S0 + NS + 2, AT_S0 + NS + 3
G_COMB, G_LN1, G_ROUTE = 0, 1, NG
G_SCAT = (NG + 1, NG + 2)


LAST = [(0, 1), (1, 3), (3, 6), (6, 8)]
LAST_PE = 6


ROUTES = [(0, 0, HT // 2), (0, HT // 2, HT), (1, 0, HT), (0, 0, HT), (1, 0, HT // 2), (1, HT // 2, HT)]
L1 = 3


def score_bank(f):
    return {1: 4, 3: 2, 5: 4}.get(f, 6)


def program(nc, x, Wq, bq, WkT, bk, Wv, bv, Wo, bo, WcT, gcen, ecen, ebias, wg, wu, wd, sg, su, sd, consts, out):
    xbuf = nc.dram_tensor("xbuf", [SLOTS, DX], F32).ap()
    ybuf = nc.dram_tensor("ybuf", [RES, D], F32).ap()
    x_t = x.rearrange("b (n p) d -> p (b n) d", p=P)
    out_t = out.rearrange("b (n p) d -> p (b n) d", p=P)

    with ExitStack() as ctx:
        def sb(name, shape, dt=F32):
            return ctx.enter_context(nc.sbuf_tensor(name, shape, dt))

        def sem(name):
            return ctx.enter_context(nc.semaphore(name))

        PS = ctx.enter_context(nc.psum_tensor("PS", [P, 8, 512], F32))

        def flat(b0, n):
            return PS[:, b0:b0 + n, :].rearrange("p b n -> p (b n)")

        cst = sb("cst", [P, C_N])
        identb = sb("identb", [P, P], BF16)
        trib = sb("trib", [P, P], BF16)
        onesb = sb("onesb", [P, P], BF16)
        causS = sb("causS", [P, P], BF16)
        xs = sb("xs", [P, NT, D])
        xn = sb("xn", [P, NT, DX])
        xnT = sb("xnT", [P, NT * P])
        cen = sb("cen", [G + E, D])
        cenn = sb("cenn", [G + E, D])
        cenT = sb("cenT", [P, G + E])
        csq = sb("csq", [G + E, 4])
        ebb = sb("ebb", [P, E])
        st = sb("st", [P, HT, 6])
        mv = sb("mv", [P, HT, 2])
        std = sb("std", [P, HT])
        rstd = sb("rstd", [P, HT])
        dev = sb("dev", [P, HT])
        table = sb("table", [1, 16])
        rn = sb("rn", [P, HT])
        gs = sb("gs", [P, HT, G])
        es = sb("es", [P, HT, E])
        v8 = sb("v8", [P, HT, 8])
        i8 = sb("i8", [P, HT, 8], U32)
        idf = sb("idf", [P, HT, K])
        eif = sb("eif", [P, HT, K])
        gm = sb("gm", [P, HT, G])
        pen = sb("pen", [P, HT, G])
        mk = sb("mk", [P, HT, E])
        sel = sb("sel", [P, NT, E], BF16)
        gd = sb("gd", [P, 2, HT, K])
        ge = sb("ge", [P, 2, HT, K])
        gsum = sb("gsum", [P, HT])
        pos = sb("pos", [P, HT * K])
        over = sb("over", [P, HT * K])
        keep = sb("keep", [P, HT * K])
        slf = sb("slf", [P, HT * K])
        gate = sb("gate", [P, 2, HT * K])
        sidx = sb("sidx", [P, 2, HT * K], I32)
        eid = sb("eid", [P, PT])
        hit = sb("hit", [P, PT, K])
        kth = sb("kth", [P, PT])
        yidx = sb("yidx", [P, 2, PT], I32)
        sgw = sb("sgw", [P, HID])
        suw = sb("suw", [P, HID])
        sdw = sb("sdw", [P, HC, D])
        yg = sb("yg", [P, HT, K, D])
        wq_in = sb("wq_in", [P, NH, HD])
        wv_in = sb("wv_in", [P, NH * LAT])
        wo_in = sb("wo_in", [P, 8, D])
        wcT = sb("wcT", [P, 2, HD])
        bk2 = sb("bk2", [P, 8, 2])
        bvc = sb("bvc", [P, 8])
        bor = sb("bor", [1, D])
        brow = sb("brow", [1, D])
        bq2 = sb("bq2", [2, NH, HD])
        wqx = sb("wqx", [P, NH, RW])
        wkx = sb("wkx", [P, NH, RW])
        bqf = sb("bqf", [2, NH, RW])
        bkf = sb("bkf", [2, NH, RW])
        bqs = sb("bqs", [2, NH * RW])
        bqx = sb("bqx", [2, NH * RW], F32R)
        bkx = sb("bkx", [2, NH * RW], F32R)
        ones2 = sb("ones2", [2, 512], F32R)
        Qn = sb("Qn", [P, T], F32R)
        Kn = sb("Kn", [P, T], F32R)
        Qc = [sb(f"Qc{i}", [P, T], F32R) for i in range(2)]
        Kz = [sb(f"Kz{i}", [P, HG, T], F32R) for i in range(2)]
        mxp = sb("mxp", [P, HT, 2, HG])
        mxm = sb("mxm", [P, HT, HG])
        M = sb("M", [P, HT, HG, RW])
        pT = sb("pT", [P, 4, 512])
        rec = sb("rec", [P, 2, 4, 1])
        area_o = sb("area_o", [P, HT * NH * LAT])
        area_v = sb("area_v", [P, HT * NH * VW + P - VW])

        def parts(area, first, *shapes):
            views, at = [], first
            for shape, pattern, sizes in shapes:
                v = area[:, at:at + shape]
                views.append(v.rearrange(pattern, **sizes) if pattern else v)
                at += shape
            assert at <= area.shape[1]
            return views

        os_ = area_o[:].rearrange("p (i n) -> p i n", i=HT)
        vs = area_v[:, 0:HT * NH * VW].rearrange("p (j h l) -> p j h l", j=HT, h=NH)
        half = ("p (c n) -> p c n", dict(c=HC))
        sil0, sil1, hb0, hb1 = parts(area_o, 0, *[(HC * 512, *half)] * 4)
        sil, hb = [sil0, sil1], [hb0, hb1]
        xeT0, xeT1 = parts(area_o, 4 * HC * 512, *[(PAIR, None, None)] * 2)
        xeT = [xeT0, xeT1]
        rows = (PAIR, "p (t d) -> p t d", dict(d=D))
        xrows = (PT * DX, "p (t d) -> p t d", dict(d=DX))
        yo0, yo1 = parts(area_o, 4 * HC * 512 + 2 * PAIR, rows, rows)
        yo = [yo0, yo1]
        yh, = parts(area_o, 0, (HT * K * D, "p (t k d) -> p t k d", dict(t=HT, k=K)))
        wkT, = parts(area_o, 0, (NH * LAT, None, None))
        wide = (2 * HID, "p (a n) -> p a n", dict(a=2))
        deep = (2 * HC * D, "p (a c n) -> p a c n", dict(a=2, c=HC))
        wgt0, wgt1, wut0, wut1, wdt0, wdt1, xe0, xe1 = parts(
            area_v, 0, wide, wide, wide, wide, deep, deep, xrows, xrows)
        wgt, wut, wdt, xe = [wgt0, wgt1], [wut0, wut1], [wdt0, wdt1], [xe0, xe1]
        oh, pc, geq = parts(yg[:].rearrange("p t k d -> p (t k d)"), 0, *[(HT * K * E, "p (n e) -> p n e", dict(e=E))] * 2,
                            (HT * KG * G, "p (n e) -> p n e", dict(e=G)))
        yT = parts(area_v, 0, (T, None, None), (T, None, None))

        s_const = sem("s_const")
        s_x = sem("s_x")
        s_cen = sem("s_cen")
        s_w = sem("s_w")
        s_zero = sem("s_zero")
        s_zero1 = sem("s_zero1")
        s_fill = sem("s_fill")
        s_filly = sem("s_filly")
        s_cst = sem("s_cst")
        s_dve = sem("s_dve")
        s_act = sem("s_act")
        s_cn = sem("s_cn")
        s_cnn = sem("s_cnn")
        s_ct = sem("s_ct")
        s_ctc = sem("s_ctc")
        s_wk = sem("s_wk")
        s_ax = sem("s_ax")
        ln_stat = sem("ln_stat")
        ln_std = sem("ln_std")
        xn_ready = sem("xn_ready")
        xnT_ps = sem("xnT_ps")
        xnT_ready = sem("xnT_ready")
        sc_ready = sem("sc_ready")
        sc_read = sem("sc_read")
        sel_ready = sem("sel_ready")
        gd_ready = sem("gd_ready")
        ge_ready = sem("ge_ready")
        cum_ready = sem("cum_ready")
        slot_ready = sem("slot_ready")
        scat = sem("scat")
        sh_gu = sem("sh_gu")
        sh_sil = sem("sh_sil")
        sh_h = sem("sh_h")
        sh_y = sem("sh_y")
        sh_x = sem("sh_x")
        w_in = [sem(f"w_in{j}") for j in range(2)]
        d_in = [sem(f"d_in{j}") for j in range(2)]
        x_in = [sem(f"x_in{j}") for j in range(2)]
        xeT_ps = sem("xeT_ps")
        xeT_sb = sem("xeT_sb")
        gu_ready = sem("gu_ready")
        sil_ready = sem("sil_ready")
        h_ready = sem("h_ready")
        y_ps = sem("y_ps")
        y_sb = sem("y_sb")
        idx_step = sem("idx_step")
        y_begun = sem("y_begun")
        y_out = [sem(f"y_out{j}") for j in range(2)]
        gath = [sem(f"gath{t}") for t in range(HT)]
        gath_h = [sem(f"gath_h{q}") for q in range(len(LAST))]
        term = sem("term")
        total = sem("total")
        last_x = sem("last_x")
        comb = sem("comb")
        v_ps = sem("v_ps")
        v_a = sem("v_a")
        v_ones = sem("v_ones")
        qk_ps = sem("qk_ps")
        tq_ready = sem("tq_ready")
        qk_split = sem("qk_split")
        kz_ready = sem("kz_ready")
        s_ready = sem("s_ready")
        smax = sem("smax")
        m_ready = sem("m_ready")
        mt_ready = sem("mt_ready")
        qc_ready = sem("qc_ready")
        st_ready = sem("st_ready")
        exp_done = sem("exp_done")
        mask_done = sem("mask_done")
        pv_done = sem("pv_done")
        norm_done = sem("norm_done")
        yt_ps = sem("yt_ps")
        yt_a = sem("yt_a")
        yt_d = sem("yt_d")
        wo_ps = sem("wo_ps")
        wo_x = sem("wo_x")
        s_out = sem("s_out")

        ident = cst[:, C_ID:C_ID + P]
        block = ctx.enter_context(nc.Block())
        N_W = 13 * 16

        @block.sync
        def _(sp):
            sp.dma_start(cst[:], consts).then_inc(s_const, 16)
            for h in range(4):
                sp.dma_start(xs[:, 4 * h:4 * h + 4, :], x_t[:, 4 * h:4 * h + 4, :]).then_inc(s_x, 16)
            sp.dma_start(cen[0:G, :], gcen).then_inc(s_cen, 16)
            sp.dma_start(cen[G:G + E, :], ecen).then_inc(s_cen, 16)
            sp.dma_start(ebb[:], ebias.partition_broadcast(P)).then_inc(s_cen, 16)
            sp.wait_ge(s_zero, 2)
            zt = Kz[0][:].rearrange("p h t -> p (h t)").bitcast(F32)
            zrow = SLOTS * DX // P // 4
            xb_flat = xbuf.rearrange("(p c) d -> p (c d)", p=P)
            for k in range(4):
                sp.dma_start(xb_flat[:, k * zrow:(k + 1) * zrow], zt[:, 0:zrow]).then_inc(s_fill, 16)
            sp.dma_start(sgw[:], sg).then_inc(s_w, 16)
            sp.dma_start(suw[:], su).then_inc(s_w, 16)
            sp.dma_start(sdw[:], sd.rearrange("(c p) d -> p c d", p=P)).then_inc(s_w, 16)
            sp.dma_start(wkT, WkT).then_inc(s_w, 16)
            sp.dma_start(wq_in[:].rearrange("p h d -> p (h d)"), Wq).then_inc(s_w, 16)
            sp.dma_start(wv_in[:], Wv).then_inc(s_w, 16)
            sp.dma_start(wo_in[:], Wo.rearrange("(c p) d -> p c d", p=P)).then_inc(s_w, 16)
            for a in range(2):
                sp.dma_start(wcT[a * LAT:(a + 1) * LAT, a, :], WcT).then_inc(s_w, 16)
            sp.dma_start(bq2[:].rearrange("a h d -> a (h d)"), bq).then_inc(s_w, 16)
            sp.dma_start(bk2[:], bk).then_inc(s_w, 16)
            sp.dma_start(bvc[:], bv).then_inc(s_w, 16)
            sp.dma_start(bor[:], bo.rearrange("(a n) -> a n", a=1)).then_inc(s_w, 16)
            yb_flat = ybuf.rearrange("(p c) d -> p (c d)", p=P)
            for k in range(2):
                sp.dma_start(yb_flat[:, k * HG * T:(k + 1) * HG * T], zt).then_inc(s_filly, 16)

            def pair_in(L, n, j):
                first = isinstance(n, int)
                if first:
                    gate_up_in(n, j)
                    down_in(n, j)
                else:
                    sp.wait_ge(h_ready, n * 4 + (4 * NPAIR * L - 2))
                sp.wait_ge(scat, 64 * 16 * (L + 1))
                sp.dma_start(xe[j], xbuf[bass.ds(n * PAIR, PAIR)].rearrange("(c p) d -> p c d", p=P)).then_inc(x_in[j], 16)
                if not first:
                    gate_up_in(n, j)
                    sp.wait_ge(y_sb, n * 2 + 2 * NPAIR * L)
                    down_in(n, j)

            def gate_up_in(n, j):
                sp.dma_start(wgt[j], wg[bass.ds(n * 2, 2)].rearrange("e p h -> p e h")).then_inc(w_in[j], 16)
                sp.dma_start(wut[j], wu[bass.ds(n * 2, 2)].rearrange("e p h -> p e h")).then_inc(w_in[j], 16)

            def down_in(n, j):
                for a in range(2):
                    sp.dma_start(wdt[j][:, a], wd[bass.ds(n * 2 + a, 1)].rearrange("e (c p) d -> p (e c) d", p=P))\
                        .then_inc(d_in[j], 16)

            def expert_pairs(L):
                for j in range(2):
                    pair_in(L, j, j)
                with sp.Fori(0, NPAIR // 2 - 1) as it:
                    for j in range(2):
                        pair_in(L, it * 2 + (j + 2), j)

            def results(L, H, t):
                if t == 0:
                    for j in range(2):
                        sp.wait_ge(y_out[j], 16 * PT * NPAIR // 2 * (L + 1))
                if 2 * L + H > 0:
                    sp.wait_ge(comb, (2 * L + H - 1) * HT + t + 1)
                tile = H * HT + t
                sp.dma_start(yg[:, t], ybuf[tile * P * K:(tile + 1) * P * K].rearrange("(p k) d -> p k d", k=K))\
                    .then_inc(gath[t], 16)

            expert_pairs(0)
            for t in range(HT):
                results(0, 0, t)
            for t in range(HT):
                results(0, 1, t)
            for Gi in range(B * NG):
                sp.wait_ge(qk_split, 2 * Gi + 2)
                sp.wait_ge(s_fill, 64)
                sp.wait_ge(s_filly, 32)
                sp.wait_ge(s_zero1, 1)
                for h in range(HG):
                    sp.dma_start(Kz[Gi % 2][RW * h:RW * h + RW, h, :].bitcast(F32),
                                 Kn[RW * h:RW * h + RW, :].bitcast(F32)).then_inc(kz_ready, 16)
            sp.wait_ge(wo_x, 2 * HT)
            expert_pairs(1)
            for q, (t0, t1) in enumerate(LAST):
                for t in range(2 * q, 2 * q + 2):
                    results(1, 0, t)
                sp.dma_start(yh[:, t0:t1], ybuf[(HT + t0) * P * K:(HT + t1) * P * K]
                             .rearrange("(t p k) d -> p t k d", k=K, p=P)).then_inc(gath_h[q], 16)
            for t in (0, 1, 2, 3, 8, 9, 10, 11, 4, 5, 6, 7, 12, 13, 14, 15):
                if HT <= t < HT + LAST_PE:
                    sp.wait_ge(last_x, t - HT + 1)
                else:
                    sp.wait_ge(comb, NT + 1 + (t if t < HT else t - LAST_PE))
                sp.dma_start(out_t[:, t, :], xs[:, t, :]).then_inc(s_out, 16)
            sp.wait_ge(s_out, 16 * NT)

        @block.gpsimd
        def _(pool):
            for k, done in enumerate((s_zero, s_zero1)):
                nc.gpsimd.memset(Kz[k][:].rearrange("p h t -> p (h t)").bitcast(F32), 0.0).then_inc(done, 1)

            def scatter(L, H, lo, hi):
                pool.wait_ge(s_fill, 16 * 4)
                for t in range(lo, hi):
                    for k in range(K):
                        scatter_one(L, H, t, k)

            def scatter_one(L, H, t, k):
                for f, route in enumerate(ROUTES):
                    if k == 0 and (L, H, t) == (f >= L1, *route[:2]):
                        pool.wait_ge(slot_ready, f + 1)
                pool.indirect_dma_start(
                    xbuf[:, :], bass.IndirectOffsetOnAxis(ap=sidx[:, H, t * K + k:t * K + k + 1], axis=0),
                    xn[:, H * HT + t, :], None, bounds_check=SLOTS - 1, oob_is_err=False).then_inc(scat, 16)

            def heads(Gi, zero):
                for n in range(SLOT):
                    N = SLOT * Gi + n
                    if n % NC in DIAG:
                        pool.wait_ge(exp_done, N + 1)
                        block_ = pT[:, N % 4, 0:P]
                        nc.gpsimd.affine_select(out=block_, in_=block_, pattern=[[1, P]], compare_op=ALU.is_ge, fill=zero,
                                                base=0, channel_multiplier=-1).then_inc(mask_done, 1)
                    elif Gi in G_SCAT:
                        tk = (Gi - G_SCAT[0]) * HG * (NC - len(DIAG)) + n // NC * (NC - len(DIAG)) + n % NC - DIAG[3] - 1
                        scatter_one(1, 0, tk // K, tk % K)

            def results(L):
                pool.wait_ge(s_filly, 32)
                if L:
                    pool.wait_ge(comb, NT)
                with pool.Fori(0, NPAIR // 2) as it:
                    for j in range(2):
                        for a, tiles in enumerate(((0, 1), (2, 3, 4))):
                            pool.wait_ge(y_sb, it * 4 + (2 * NPAIR * L + 2 * j + a + 3))
                            pool.sem_inc(y_begun, 1)
                            for t in tiles:
                                pool.indirect_dma_start(
                                    ybuf[:, :], bass.IndirectOffsetOnAxis(ap=yidx[:, j, t:t + 1], axis=0),
                                    yo[j][:, t, :], None, bounds_check=RES - 1, oob_is_err=False).then_inc(y_out[j], 16)

            scatter(0, 0, 0, HT)
            scatter(0, 1, 0, HT)
            results(0)
            zero = pool.to_reg(0.0)
            for Gi in range(B * NG):
                heads(Gi, zero)
            scatter(1, 1, 0, HT)
            results(1)

        @block.scalar
        def _(act):
            act.wait_ge(s_const, 16)
            act.wait_ge(s_cen, 48)
            nc.scalar.activation(cenn[:], cen[:], ACT.Square, accum_out=csq[:, 0:1]).then_inc(s_act, 1)
            act.wait_ge(s_act, 1)
            nc.scalar.activation(csq[:, 1:2], csq[:, 0:1], ACT.Sqrt).then_inc(s_cn, 1)

            n_tables = [0]

            def load_table(function):
                nc.scalar.activation(table[:, n_tables[0]:n_tables[0] + 1], cst[0:1, C_ONE:C_ONE + 1], function)
                n_tables[0] += 1

            def ln_std_dev(r):
                load_table(ACT.Sqrt)
                act.wait_ge(ln_stat, r + 1)
                nc.scalar.activation(std[:], mv[:, :, 1], ACT.Sqrt, bias=cst[:, C_EPS:C_EPS + 1])
                nc.scalar.activation(dev[:], mv[:, :, 1], ACT.Sqrt, scale=float(D)).then_inc(ln_std, 1)

            def ln_scaled(r, H):
                for q in range(2):
                    act.wait_ge(xnT_ps, 2 * r + q + 1)
                    nc.scalar.activation(xnT[:, H * T + 512 * q:H * T + 512 * q + 512], PS[:, q, :], ACT.Copy)\
                        .then_inc(xnT_ready, 1)

            def gates(f):
                H, a, b = ROUTES[f]
                load_table(ACT.Exp)
                act.wait_ge(gd_ready, f + 1)
                nc.scalar.activation(ge[:, H, a:b], gd[:, H, a:b], ACT.Exp).then_inc(ge_ready, 1)

            def shared(L):
                load_table(ACT.Silu)
                for q in range(4):
                    for c in range(HC):
                        n = 8 * L + 2 * q + c
                        act.wait_ge(sh_gu, n + 1)
                        if n >= 4:
                            act.wait_ge(sh_h, n - 3)
                        nc.scalar.activation(sil[q % 2][:, c, :], PS[:, 2 + c, :], ACT.Silu).then_inc(sh_sil, 1)

            def experts(L):
                turned(L, 0, 0)
                with act.Fori(0, NPAIR // 2 - 1) as it:
                    for j in range(2):
                        pair(L, it, j)
                for j in range(2):
                    pair(L, NPAIR // 2 - 1, j)

            def turned(L, it, j):
                act.wait_ge(xeT_ps, it * 2 + (NPAIR * L + j + 1))
                nc.scalar.activation(xeT[j][:], flat(0, 2)[:, 0:PAIR], ACT.Copy).then_inc(xeT_sb, 1)

            def pair(L, it, j):
                for a in range(2):
                    for c in range(HC):
                        act.wait_ge(gu_ready, it * 8 + (4 * NPAIR * L + 4 * j + 2 * a + c + 1))
                        act.wait_ge(h_ready, it * 8 + (4 * NPAIR * L + 4 * j + 2 * a + c + 1))
                        nc.scalar.activation(sil[a][:, c, 0:CAP], PS[:, 2 + c, 0:CAP], ACT.Silu).then_inc(sil_ready, 1)
                if not (isinstance(it, int) and j):
                    turned(L, it + j, 1 - j)

            def q_round(Gi):
                act.wait_ge(qk_ps, 2 * Gi + 1)
                if Gi:
                    act.wait_ge(qc_ready, Gi)
                nc.scalar.activation(Qn[:], flat(0, 2), ACT.Identity, scale=cst[:, C_SQ:C_SQ + 1]).then_inc(tq_ready, 1)

            def k_round(Gi):
                act.wait_ge(qk_ps, 2 * Gi + 2)
                if Gi:
                    act.wait_ge(kz_ready, 16 * HG * Gi)
                nc.scalar.activation(Kn[:], flat(2, 2), ACT.Identity, scale=cst[:, C_SK:C_SK + 1]).then_inc(tq_ready, 1)

            def values(b):
                if b:
                    act.wait_ge(wo_ps, HT)
                for j in range(HT):
                    if b and j == 2:
                        ln_std_dev(4)
                    if b and j == 4:
                        ln_scaled(4, 0)
                    act.wait_ge(v_ps, HT * b + j + 1)
                    nc.scalar.activation(vs[:, j, :, 0:LAT], flat(4 + 2 * (j % 2), 2).rearrange("p (h l) -> p h l", l=LAT),
                                         ACT.Copy).then_inc(v_a, 1)

            def heads(Gi):
                if Gi == G_LN1:
                    ln_std_dev(3)
                for n in range(SLOT):
                    N = SLOT * Gi + n
                    if n == AT_QK + 1 and Gi + 1 < B * NG:
                        q_round(Gi + 1)
                    if n == AT_QK + 2 and Gi + 1 < B * NG:
                        k_round(Gi + 1)
                    if n == AT_TR + 1 and Gi == G_LN1:
                        ln_scaled(3, 1)
                    if n == AT_CNT and Gi == G_ROUTE:
                        gates(L1)
                    w = CHUNKS[n % NC][2]
                    act.wait_ge(st_ready, N + 1)
                    if N >= 4:
                        act.wait_ge(pv_done, N - 3)
                    nc.scalar.activation(pT[:, N % 4, 0:w], PS[:, 4 + N % 2, 0:w], ACT.Exp).then_inc(exp_done, 1)

            def out_rows(b):
                for i in range(HT):
                    n = HT * b + i
                    act.wait_ge(yt_ps, n + 1)
                    if n >= 2:
                        act.wait_ge(wo_ps, n - 1)
                    nc.scalar.activation(yT[i % 2][:, 0:512], PS[:, 2 * (i % 2), :], ACT.Copy).then_inc(yt_a, 1)

            for H in range(2):
                ln_std_dev(H)
                ln_scaled(H, H)
                for f in ((0, 1), (2,))[H]:
                    gates(f)
            shared(0)
            experts(0)
            ln_std_dev(2)
            ln_scaled(2, 0)
            for b in range(B):
                if b == 0:
                    q_round(0)
                    k_round(0)
                    load_table(ACT.Exp)
                values(b)
                for g in range(NG):
                    heads(NG * b + g)
                out_rows(b)
            ln_std_dev(5)
            ln_scaled(5, 1)
            for f in (4, 5):
                gates(f)
            shared(1)
            experts(1)
            for t in range(LAST_PE + 1):
                if t < LAST_PE:
                    if t in dict(LAST):
                        act.wait_ge(gath_h[[t0 for t0, t1 in LAST].index(t)], 16)
                    for k in range(K):
                        ins = nc.scalar.activation(yh[:, t, k, :], yh[:, t, k, :], ACT.Copy,
                                                   scale=gate[:, 1, t * K + k:t * K + k + 1])
                    ins.then_inc(term, 1)
                if t:
                    act.wait_ge(total, t)
                    nc.scalar.activation(xs[:, HT + t - 1, :], PS[:, (t - 1) % 4, 0:D], ACT.Copy).then_inc(last_x, 1)

        @block.vector
        def _(dve):
            n_dve = [0]

            def link(ins):
                n_dve[0] += 1
                ins.then_inc(s_dve, 1)
                dve.wait_ge(s_dve, n_dve[0])

            tt, ts, stt = nc.vector.tensor_tensor, nc.vector.tensor_scalar, nc.vector.scalar_tensor_tensor
            nc.vector.memset(wcT[:], 0.0).then_inc(s_zero, 1)
            nc.vector.memset(M[:], 0.0)
            nc.vector.memset(mxp[:], -3.0e38)
            nc.vector.memset(wqx[:], 0.0)
            nc.vector.memset(wkx[:], 0.0)
            nc.vector.memset(bqf[:], 0.0)
            link(nc.vector.memset(bkf[:], 0.0))
            nc.vector.memset(bkf[:, :, 0:R0], 1.0)
            nc.vector.memset(ones2[:].bitcast(F32), 1.0)
            nc.vector.memset(xn[:, :, D:DX], 0.0)
            nc.vector.memset(st[:], 0.0)
            nc.vector.memset(mv[:], 0.0).then_inc(h_ready, 2)
            nc.vector.memset(rn[:], 0.0).then_inc(y_sb, 2)
            nc.vector.memset(rec[:], 0.0).then_inc(y_ps, 2)
            nc.vector.memset(gsum[:], 0.0)
            nc.vector.memset(mxm[:], 0.0)
            dve.wait_ge(s_const, 16)
            nc.vector.tensor_copy(identb[:], ident)
            nc.vector.tensor_copy(trib[:], cst[:, C_TRI:C_TRI + P])
            nc.vector.tensor_copy(onesb[:], cst[:, C_ONE:C_ONE + P])
            link(nc.vector.tensor_copy(causS[:], cst[:, C_CS:C_CS + P]))
            nc.vector.memset(rstd[:], 0.0).then_inc(s_cst, 1)
            dve.wait_ge(s_cn, 1)
            link(ts(csq[:, 2:3], csq[:, 1:2], 1e-12, None, ALU.max))
            link(nc.vector.reciprocal(csq[:, 3:4], csq[:, 2:3]))
            ts(cenn[:], cen[:], csq[:, 3:4], None, ALU.mult).then_inc(s_cnn, 1)
            dve.wait_ge(s_ct, 1)
            nc.vector.tensor_copy(cenT[:], PS[:, 6, 0:G + E]).then_inc(s_ctc, 1)

            def fold():
                dve.wait_ge(s_w, N_W)
                dve.wait_ge(s_wk, 1)
                for r in range(3):
                    c = slice(R0 + HD * r, R0 + HD * r + HD)
                    ts(wqx[:, :, c], wq_in[:], SCALE, None, ALU.mult)
                    ts(bqf[:, :, c], bq2[:], SCALE, None, ALU.mult)
                    nc.vector.tensor_copy(wkx[:, :, c], PS[:, 6, 0:P].rearrange("p (h d) -> p h d", d=HD))
                    link(nc.vector.tensor_copy(bkf[:, :, c], PS[0:2, 7, 0:P].rearrange("p (h d) -> p h d", d=HD)))
                nc.vector.tensor_copy(brow[:], PS[0:1, 7, P:2 * P])
                for src, dst in ((bqf, bqx), (bkf, bkx)):
                    f = src[:].rearrange("p h r -> p (h r)")
                    link(ts(bqs[:].bitcast(F32R), f, cst[0:2, C_S2:C_S2 + 1], None, ALU.mult))
                    link(stt(dst[:], f, cst[0:2, C_L2:C_L2 + 1], bqs[:], ALU.mult, ALU.add))
                nc.vector.memset(rstd[:], 0.0).then_inc(s_ax, 1)

            def ln(r, H):
                t0 = H * HT
                if r != 5:
                    for t in range(HT):
                        ins = nc.vector.bn_stats(st[:, t, :], xs[:, t0 + t, :])
                    link(ins)
                for t in range(HT):
                    ins = nc.vector.bn_aggr(mv[:, t, :], st[:, t, :])
                ins.then_inc(ln_stat, 1)
                dve.wait_ge(ln_std, r + 1)
                link(nc.vector.reciprocal(rstd[:], std[:]))
                link(tt(rn[:], dev[:], rstd[:], ALU.mult))
                link(ts(rn[:], rn[:], 1e-12, None, ALU.max))
                nc.vector.reciprocal(rn[:], rn[:])
                if r >= 2:
                    dve.wait_ge(scat, 64 * 16)
                for t in range(HT):
                    ts(xn[:, t0 + t, 0:D], xs[:, t0 + t, :], mv[:, t, 0:1], rstd[:, t:t + 1], ALU.subtract, ALU.mult)\
                        .then_inc(xn_ready, 1)

            def route_scores(f):
                H, a, b = ROUTES[f]
                n = b - a
                bank = score_bank(f)
                dve.wait_ge(sc_ready, f + 1)
                sc = PS[:, bank, a * (G + E):b * (G + E)].rearrange("p (t n) -> p t n", n=G + E)
                link(tt(gs[:, a:b], sc[:, :, 0:G], rn[:, a:b].unsqueeze(2).broadcast_to([P, n, G]), ALU.mult))
                tt(es[:, a:b], sc[:, :, G:G + E], rn[:, a:b].unsqueeze(2).broadcast_to([P, n, E]), ALU.mult).then_inc(sc_read, 1)

            def route_groups(f):
                H, a, b = ROUTES[f]
                n = b - a
                dve.wait_ge(sc_read, f + 1)
                link(tt(es[:, a:b], es[:, a:b], ebb[:].unsqueeze(1).broadcast_to([P, n, E]), ALU.add))
                for t in range(a, b):
                    ins = nc.vector.max(v8[:, t, :], gs[:, t, :])
                link(ins)
                for t in range(a, b):
                    ins = nc.vector.max_index(i8[:, t, :], v8[:, t, :], gs[:, t, :])
                link(ins)
                link(nc.vector.tensor_copy(idf[:, a:b], i8[:, a:b, 0:KG]))
                link(tt(geq[:, a * KG:b * KG], cst[:, C_I8:C_I8 + G].unsqueeze(1).broadcast_to([P, n * KG, G]),
                        idf[:, a:b].rearrange("p t k -> p (t k)").unsqueeze(2).broadcast_to([P, n * KG, G]), ALU.is_equal))
                link(nc.vector.tensor_reduce(gm[:, a:b], geq[:, a * KG:b * KG].rearrange("p (t k) g -> p t g k", k=KG), AX.X, ALU.add))
                ts(pen[:, a:b], gm[:, a:b], 1.0e9, -1.0e9, ALU.mult, ALU.add)
                gmf = gm[:, a:b].rearrange("p t g -> p (t g)").unsqueeze(2).broadcast_to([P, n * G, EG])
                pnf = pen[:, a:b].rearrange("p t g -> p (t g)").unsqueeze(2).broadcast_to([P, n * G, EG])
                mkf = mk[:, a:b].rearrange("p t (g e) -> p (t g) e", e=EG)
                link(tt(mkf, es[:, a:b].rearrange("p t (g e) -> p (t g) e", e=EG), gmf, ALU.mult))
                link(tt(mkf, mkf, pnf, ALU.add))

            def route_experts(f):
                H, a, b = ROUTES[f]
                n = b - a
                for t in range(a, b):
                    ins = nc.vector.max(v8[:, t, :], mk[:, t, :])
                link(ins)
                tt(gd[:, H, a:b], v8[:, a:b, 0:K], v8[:, a:b, 0:1].broadcast_to([P, n, K]), ALU.subtract).then_inc(gd_ready, 1)
                for t in range(a, b):
                    ins = nc.vector.max_index(i8[:, t, :], v8[:, t, :], mk[:, t, :])
                link(ins)
                link(nc.vector.tensor_copy(eif[:, a:b], i8[:, a:b, 0:K]))

            def route_hot(f):
                H, a, b = ROUTES[f]
                n = b - a
                link(tt(oh[:, a * K:b * K], cst[:, C_I32:C_I32 + E].unsqueeze(1).broadcast_to([P, n * K, E]),
                        eif[:, a:b].rearrange("p t k -> p (t k)").unsqueeze(2).broadcast_to([P, n * K, E]), ALU.is_equal))
                with nc.allow_low_precision("zeros and ones"):
                    nc.vector.tensor_reduce(sel[:, H * HT + a:H * HT + b, :], oh[:, a * K:b * K].rearrange("p (t k) e -> p t e k", k=K),
                                            AX.X, ALU.add).then_inc(sel_ready, 1)

            def route_slots(f):
                H, a, b = ROUTES[f]
                n = b - a
                dve.wait_ge(ge_ready, f + 1)
                link(nc.vector.tensor_reduce(gsum[:, a:b], ge[:, H, a:b], AX.X, ALU.add))
                link(nc.vector.reciprocal(gsum[:, a:b], gsum[:, a:b]))
                tt(ge[:, H, a:b], ge[:, H, a:b], gsum[:, a:b].unsqueeze(2).broadcast_to([P, n, K]), ALU.mult)
                dve.wait_ge(cum_ready, f + 1)
                cnt = PS[:, score_bank(f) + 1, (H * HT + a) * E:(H * HT + b) * E].rearrange("p (t e) -> p t e", e=E)
                link(tt(pc[:, a * K:b * K].rearrange("p (t k) e -> p t k e", k=K), oh[:, a * K:b * K].rearrange("p (t k) e -> p t k e", k=K),
                        cnt.unsqueeze(2).broadcast_to([P, n, K, E]), ALU.mult))
                link(nc.vector.tensor_reduce(pos[:, a * K:b * K], pc[:, a * K:b * K], AX.X, ALU.add))
                ts(over[:, a * K:b * K], pos[:, a * K:b * K], float(CAP), float(SKIP), ALU.is_gt, ALU.mult)
                ts(keep[:, a * K:b * K], pos[:, a * K:b * K], float(CAP), 0.5, ALU.is_le, ALU.mult)
                link(stt(slf[:, a * K:b * K], eif[:, a:b].rearrange("p t k -> p (t k)"), float(CAP), pos[:, a * K:b * K], ALU.mult, ALU.add))
                nc.vector.tensor_copy(xn[:, H * HT + a:H * HT + b, X_EXP:X_EXP + K], eif[:, a:b])
                ts(xn[:, H * HT + a:H * HT + b, X_TOK], cst[:, C_TOK + H * HT + a:C_TOK + H * HT + b],
                   float(LAYER if f >= L1 else 0), None, ALU.add)
                link(tt(gate[:, H, a * K:b * K], ge[:, H, a:b].rearrange("p t k -> p (t k)"), keep[:, a * K:b * K], ALU.mult))
                stt(sidx[:, H, a * K:b * K], slf[:, a * K:b * K], -1.0, over[:, a * K:b * K], ALU.add, ALU.add).then_inc(slot_ready, 1)

            def shared(L):
                for q in range(4):
                    for c in range(HC):
                        n = 8 * L + 2 * q + c
                        dve.wait_ge(sh_sil, n + 1)
                        if n >= 4:
                            dve.wait_ge(sh_y, (n - 4) // 2 + 1)
                        tt(hb[q % 2][:, c, :], sil[q % 2][:, c, :], PS[:, 4 + c, :], ALU.mult).then_inc(sh_h, 1)
                    if q:
                        shared_x(L, q - 1)
                shared_x(L, 3)

            def shared_x(L, q):
                dve.wait_ge(sh_y, 4 * L + q + 1)
                xq = xs[:, 4 * q:4 * q + 4, :].rearrange("p t d -> p (t d)")
                stt(xq, PS[:, 6 + q % 2, :], 0.5, xq, ALU.mult, ALU.add).then_inc(sh_x, 1)

            def result_rows(L, it, j):
                def step(i):
                    return it * 8 + (4 * NPAIR * L + 4 * j + i)
                dve.wait_ge(x_in[j], it * 16 + (16 * NPAIR // 2 * L + 16))
                tt(hit[:], xe[j][:, :, X_EXP:X_EXP + K], eid[:].unsqueeze(2).broadcast_to([P, PT, K]), ALU.is_equal)\
                    .then_inc(idx_step, 1)
                dve.wait_ge(idx_step, step(1))
                ts(eid[:], eid[:], 2.0, None, ALU.add)
                tt(hit[:], hit[:], cst[:, C_K:C_K + K].unsqueeze(1).broadcast_to([P, PT, K]), ALU.mult).then_inc(idx_step, 1)
                dve.wait_ge(idx_step, step(2))
                nc.vector.tensor_reduce(kth[:], hit[:], AX.X, ALU.add).then_inc(idx_step, 1)
                dve.wait_ge(idx_step, step(3))
                if L or not isinstance(it, int) or it:
                    dve.wait_ge(y_out[j], it * (16 * PT) + 16 * PT * NPAIR // 2 * L)
                stt(yidx[:, j, :], kth[:], float(LAYER * (L + 1)), xe[j][:, :, X_TOK], ALU.add, ALU.subtract)\
                    .then_inc(idx_step, 1)
                dve.wait_ge(idx_step, step(4))

            def experts(L):
                link(nc.vector.tensor_copy(eid[:], cst[:, C_EID:C_EID + PT]))
                two_pairs(L, 0)
                with dve.Fori(0, NPAIR // 2 - 1) as it:
                    two_pairs(L, it + 1)

            def two_pairs(L, it):
                for j in range(2):
                    result_rows(L, it, j)
                    for a in range(2):
                        for c in range(HC):
                            dve.wait_ge(sil_ready, it * 8 + (4 * NPAIR * L + 4 * j + 2 * a + c + 1))
                            if c == 0:
                                dve.wait_ge(y_ps, it * 4 + (2 * NPAIR * L + 2 * j + a) + 1)
                            tt(hb[a][:, c, 0:CAP], sil[a][:, c, 0:CAP], PS[:, 4 + c, 0:CAP], ALU.mult)\
                                .then_inc(h_ready, 1)
                    for a in range(2):
                        dve.wait_ge(y_ps, it * 4 + (2 * NPAIR * L + 2 * j + a + 3))
                        ya = PS[:, 6 + a, 0:3 * D].rearrange("p (t d) -> p t d", d=D)
                        if a == 0:
                            nc.vector.tensor_copy(yo[j][:, 0:2, :], ya[:, 0:2, :])
                            nc.vector.tensor_copy(yo[j][0:64, 2, :], ya[0:64, 2, :]).then_inc(y_sb, 1)
                        else:
                            nc.vector.tensor_copy(yo[j][64:P, 2, :], ya[64:P, 0, :])
                            nc.vector.tensor_copy(yo[j][:, 3:5, :], ya[:, 1:3, :]).then_inc(y_sb, 1)

            def combine(L, H):
                for t0 in range(0, HT, 4):
                    combine_tiles(H, yg, range(t0, t0 + 4), lambda t: dve.wait_ge(gath[t], 16 * (2 * L + H + 1)))
                dve.wait_ge(comb, HT * (2 * L + H + 1))

            def combine_tiles(H, y, tiles, wait_results):
                n, first = len(tiles), n_dve[0] + 1
                for k in range(K):
                    for i, t in enumerate(tiles):
                        if k == 0:
                            wait_results(t)
                        else:
                            dve.wait_ge(s_dve, first + n * (k - 1) + i)
                        xt = xs[:, H * HT + t, :]
                        ins = stt(xt, y[:, t, k, :], gate[:, H, t * K + k:t * K + k + 1], xt, ALU.mult, ALU.add)
                        if k < K - 1:
                            ins.then_inc(s_dve, 1)
                            n_dve[0] += 1
                        else:
                            ins.then_inc(comb, 1)

            def qk_parts(Gi):
                for q, (dst, col) in enumerate(((Qn, C_LQ), (Kn, C_LK))):
                    dve.wait_ge(tq_ready, 2 * Gi + q + 1)
                    stt(dst[:], flat(2 * q, 2), cst[:, col:col + 1], dst[:].bitcast(F32), ALU.mult, ALU.add)\
                        .then_inc(qk_split, 1)

            def row_max(Gi, s):
                i, c, w = ROWS[s // 2]
                hp = s % 2
                dve.wait_ge(s_ready, NS * Gi + s + 1)
                nc.vector.tensor_reduce(mxp[:, i, c, 2 * hp:2 * hp + 2], PS[:, 2 * hp:2 * hp + 2, 0:w], AX.X, ALU.max)\
                    .then_inc(smax, 1)

            def max_parts(Gi):
                dve.wait_ge(smax, NS * Gi + NS)
                link(tt(mxm[:], mxp[:, :, 0, :], mxp[:, :, 1, :], ALU.max))
                if Gi:
                    dve.wait_ge(mt_ready, Gi)
                link(ts(M[:, :, :, 0].bitcast(F32R), mxm[:], -1.0, None, ALU.mult))
                stt(M[:, :, :, 1].bitcast(F32R), mxm[:], -1.0, M[:, :, :, 0], ALU.mult, ALU.subtract)\
                    .then_inc(m_ready, 1)

            def q_with_max(Gi):
                dve.wait_ge(mt_ready, Gi + 1)
                tt(Qc[Gi % 2][:], flat(0, 2), Qn[:].bitcast(F32), ALU.add).then_inc(qc_ready, 1)

            def normalise(Gi, hh, half):
                X = HG * Gi + hh
                dve.wait_ge(pv_done, SLOT * Gi + NC * hh + (4 if half == 0 else NC))
                o = PS[:, 6 + half, :].rearrange("p (t l) -> p t l", l=P)
                link(nc.vector.reciprocal(rec[:, half], o[:, :, LAT:VW]))
                h = (Gi % NG) * HG + hh
                tt(os_[:, 4 * half:4 * half + 4, h * LAT:(h + 1) * LAT], o[:, :, 0:LAT],
                   rec[:, half].broadcast_to([P, 4, LAT]), ALU.mult).then_inc(norm_done, 1)

            def value_ones(b):
                if b:
                    dve.wait_ge(wo_ps, HT)
                nc.vector.memset(area_v[:, HT * NH * VW:], 0.0)
                nc.vector.memset(vs[:, :, :, LAT:VW], 1.0).then_inc(v_ones, 1)

            def heads(Gi):
                if Gi == G_LN1:
                    ln(3, 1)
                for n in range(SLOT):
                    if n % NC == 7:
                        normalise(Gi, n // NC, 0)
                    if n % NC == 3 and n > NC:
                        normalise(Gi, n // NC - 1, 1)
                    if Gi + 1 < B * NG:
                        if n == AT_SPLIT:
                            qk_parts(Gi + 1)
                        if AT_S0 <= n < AT_MAX:
                            row_max(Gi + 1, n - AT_S0)
                        if n == AT_MAX:
                            max_parts(Gi + 1)
                        if n == AT_QC:
                            q_with_max(Gi + 1)
                    if n == AT_COMB and Gi == G_COMB:
                        combine(0, 1)
                    if n == AT_SLOTS and Gi == G_ROUTE:
                        route_slots(L1)
                normalise(Gi, HG - 1, 1)

            def out_rows(b):
                for i in range(HT):
                    n = HT * b + i
                    dve.wait_ge(yt_ps, n + 1)
                    if n >= 2:
                        dve.wait_ge(wo_ps, n - 1)
                    nc.vector.tensor_copy(yT[i % 2][:, 512:1024], PS[:, 2 * (i % 2) + 1, :]).then_inc(yt_d, 1)
                    if i:
                        add_x(b, i - 1)
                    if b and i > 1:
                        stats(i - 2)
                add_x(b, HT - 1)
                dve.wait_ge(wo_x, HT * (b + 1))
                if b:
                    stats(HT - 2)
                    link(stats(HT - 1))

            def stats(i):
                dve.wait_ge(wo_x, HT + i + 1)
                return nc.vector.bn_stats(st[:, i, :], xs[:, HT + i, :])

            def add_x(b, i):
                dve.wait_ge(wo_ps, HT * b + i + 1)
                xt = xs[:, HT * b + i, :]
                tt(xt, PS[:, 6 + i % 2, 0:D], xt, ALU.add).then_inc(wo_x, 1)

            route_steps = (route_scores, route_groups, route_experts, route_hot, route_slots)
            dve.wait_ge(s_x, 64)
            for H in range(2):
                ln(H, H)
                for f in ((0, 1), (2,))[H]:
                    for step in route_steps:
                        step(f)
            fold()
            shared(0)
            experts(0)
            combine(0, 0)
            ln(2, 0)
            for b in range(B):
                value_ones(b)
                if b:
                    ln(4, 0)
                    for step in route_steps[:-1]:
                        step(L1)
                if b == 0:
                    qk_parts(0)
                    for s in range(NS):
                        row_max(0, s)
                    max_parts(0)
                    q_with_max(0)
                for g in range(NG):
                    heads(NG * b + g)
                out_rows(b)
            ln(5, 1)
            for f in (4, 5):
                for step in route_steps:
                    step(f)
            shared(1)
            experts(1)
            combine(1, 0)
            combine_tiles(1, yh, range(LAST_PE, HT), lambda t: dve.wait_ge(gath_h[-1], 16))

        @block.tensor
        def _(pe):
            mm = nc.tensor.matmul

            def ln(r, H):
                for q in range(2):
                    for t in range(4):
                        tile = 4 * q + t
                        pe.wait_ge(xn_ready, HT * r + tile + 1)
                        ins = nc.tensor.transpose(PS[:, q, t * P:(t + 1) * P], xn[:, H * HT + tile, 0:D], ident)
                    ins.then_inc(xnT_ps, 1)

            def scores(f, r):
                H, a, b = ROUTES[f]
                pe.wait_ge(xnT_ready, 2 * r + (1 if b < HT else 2))
                for t in range(a, b):
                    c0 = (H * HT + t) * P
                    ins = mm(PS[:, score_bank(f), t * (G + E):(t + 1) * (G + E)], xnT[:, c0:c0 + P], cenT[:], start=True, stop=True)
                ins.then_inc(sc_ready, 1)

            def counts(f):
                H, t0, t1 = ROUTES[f]
                t0, t1 = H * HT + t0, H * HT + t1

                def cols(a, b):
                    return PS[:, score_bank(f) + 1, a * E:b * E]
                for j in range(t1 - 1):
                    if j == t0:
                        pe.wait_ge(sel_ready, f + 1)
                    a = max(j + 1, t0)
                    mm(cols(a, t1).rearrange("p (t e) -> p t e", e=E), onesb[:],
                       sel[:, j:j + 1, :].broadcast_to([P, t1 - a, E]), start=(j == 0), stop=False, skip_group_check=True)
                mm(cols(t0, t1), trib[:], sel[:, t0:t1, :].rearrange("p t e -> p (t e)"), start=False, stop=True,
                   skip_group_check=True).then_inc(cum_ready, 1)

            def shared(L):
                def down(q):
                    pe.wait_ge(sh_h, 8 * L + 2 * q + 2)
                    if q >= 2:
                        pe.wait_ge(sh_x, 4 * L + q - 1)
                    for c in range(HC):
                        for t in range(4):
                            ins = mm(PS[:, 6 + q % 2, t * D:(t + 1) * D], hb[q % 2][:, c, t * P:(t + 1) * P], sdw[:, c, :],
                                     start=(c == 0 and t == 0), stop=(c == HC - 1), skip_group_check=True)
                    ins.then_inc(sh_y, 1)

                for q in range(4):
                    for c in range(HC):
                        n = 8 * L + 2 * q + c
                        if q:
                            pe.wait_ge(sh_h, n - 1)
                        rhs = xnT[:, 512 * q:512 * q + 512]
                        mm(PS[:, 2 + c, :], sgw[:, c * P:(c + 1) * P], rhs, start=True, stop=True)
                        mm(PS[:, 4 + c, :], suw[:, c * P:(c + 1) * P], rhs, start=True, stop=True).then_inc(sh_gu, 1)
                    if q:
                        down(q - 1)
                down(3)

            def experts(L):
                pe.wait_ge(sh_x, 4 * L + 4)
                turn(L, 0, 0)
                with pe.Fori(0, NPAIR // 2 - 1) as it:
                    for j in range(2):
                        pair(L, it, j)
                for j in range(2):
                    pair(L, NPAIR // 2 - 1, j)

            def turn(L, it, j):
                pe.wait_ge(x_in[j], it * 16 + (16 * NPAIR // 2 * L + 16))
                for t in range(PT):
                    ins = nc.tensor.transpose(flat(0, 2)[:, t * P:(t + 1) * P], xe[j][:, t, 0:D], ident)
                ins.then_inc(xeT_ps, 1)

            def pair(L, it, j):
                pe.wait_ge(w_in[j], it * 32 + (32 * NPAIR // 2 * L + 32))
                pe.wait_ge(xeT_sb, it * 2 + (NPAIR * L + j + 1))
                for a in range(2):
                    gate_up(L, it, j, a)
                pe.wait_ge(d_in[j], it * 32 + (32 * NPAIR // 2 * L + 32))
                down(L, it, j, 0)
                if not (isinstance(it, int) and j):
                    turn(L, it + j, 1 - j)
                down(L, it, j, 1)

            def gate_up(L, it, j, a):
                rhs = xeT[j][:, a * CAP:(a + 1) * CAP]
                for c in range(HC):
                    pe.wait_ge(h_ready, it * 8 + (4 * NPAIR * L + 4 * j + 2 * a + c + 1))
                    mm(PS[:, 2 + c, 0:CAP], wgt[j][:, a, c * P:(c + 1) * P], rhs, start=True, stop=True)
                    mm(PS[:, 4 + c, 0:CAP], wut[j][:, a, c * P:(c + 1) * P], rhs, start=True, stop=True)\
                        .then_inc(gu_ready, 1)

            def down(L, it, j, a):
                pe.wait_ge(y_sb, it * 4 + (2 * NPAIR * L + 2 * j + a + 1))
                tiles = ((0, P, 0, 0), (P, P, 0, 1), (2 * P, 64, 0, 2)) if a == 0 else \
                    ((64, P, 0, 1), (64 + P, P, 0, 2), (0, 64, 64, 0))
                for c in range(HC):
                    pe.wait_ge(h_ready, it * 8 + (4 * NPAIR * L + 4 * j + 2 * a + c + 3))
                    for n, (col, m, p0, t) in enumerate(tiles):
                        ins = mm(PS[p0:p0 + m, 6 + a, t * D:(t + 1) * D], hb[a][:, c, col:col + m], wdt[j][:, a, c, :],
                                 start=(c == 0 and n == 0) , stop=(c == HC - 1), skip_group_check=True)
                ins.then_inc(y_ps, 1)

            def value_half(b, j, c):
                if j >= 2 and c == 0:
                    pe.wait_ge(v_a, HT * b + j - 1)
                ins = mm(PS[:, 4 + 2 * (j % 2) + c, :], xnT[:, (HT * b + j) * P:(HT * b + j + 1) * P],
                         wv_in[:, 512 * c:512 * c + 512], start=True, stop=True)
                if c:
                    ins.then_inc(v_ps, 1)

            def value_tile(b, j):
                value_half(b, j, 0)
                value_half(b, j, 1)

            def qk(Gi):
                b, g = Gi // NG, Gi % NG
                if Gi:
                    pe.wait_ge(qc_ready, Gi)
                if Gi == G_ROUTE + 1:
                    pe.wait_ge(xnT_ready, 10)
                    pe.wait_ge(sc_read, 4)
                if Gi == G_LN1 + 2:
                    pe.wait_ge(xnT_ready, 8)
                gc = slice(g * HG * RW, (g + 1) * HG * RW)
                for q, (w, bias) in enumerate(((wqx, bqx), (wkx, bkx))):
                    for c in range(2):
                        o = PS[:, 2 * q + c, :]
                        mm(o, w[:].rearrange("p h r -> p (h r)")[:, gc], xnT[:, b * T + 512 * c:b * T + 512 * c + 512],
                           start=True, stop=False)
                        ins = mm(o, bias[:, gc], ones2[:], start=False, stop=True)
                    ins.then_inc(qk_ps, 1)

            def s_rows(Gi, s):
                i, c, w = ROWS[s // 2]
                hp = s % 2
                if s == 0:
                    if Gi == G_LN1 + 1:
                        pe.wait_ge(xnT_ready, 8)
                    if Gi == G_ROUTE + 1:
                        pe.wait_ge(slot_ready, 4)
                    pe.wait_ge(qk_split, 2 * Gi + 2)
                    pe.wait_ge(kz_ready, 16 * HG * (Gi + 1))
                if s >= 2:
                    pe.wait_ge(smax, NS * Gi + s - 1)
                diag = c == i // 4
                for hh in range(2):
                    ins = mm(PS[:, 2 * hp + hh, 0:w], Qn[:, i * P:(i + 1) * P],
                             Kz[Gi % 2][:, 2 * hp + hh, 512 * c:512 * c + w], start=True, stop=not diag)
                for hh in range(2 if diag else 0):
                    ins = mm(PS[:, 2 * hp + hh, w - P:w], identb[:], causS[:], start=False, stop=True)
                ins.then_inc(s_ready, 1)

            def max_rows(Gi):
                pe.wait_ge(m_ready, Gi + 1)
                for i in range(HT):
                    ins = nc.tensor.transpose(flat(0, 2)[:, i * P:(i + 1) * P], M[:, i].rearrange("p h r -> p (h r)"), ident)
                ins.then_inc(mt_ready, 1)

            def s_cols(Gi, n):
                N = SLOT * Gi + n
                j, t0, w, _ = CHUNKS[n % NC]
                if N >= 2:
                    pe.wait_ge(exp_done, N - 1)
                mm(PS[:, 4 + N % 2, 0:w], Kz[Gi % 2][:, n // NC, j * P:(j + 1) * P], Qc[Gi % 2][:, t0:t0 + w],
                   start=True, stop=True).then_inc(st_ready, 1)

            def pv(Gi, n):
                N = SLOT * Gi + n
                j, t0, w, half = CHUNKS[n % NC]
                X = HG * Gi + n // NC
                first = n % NC == (0 if half == 0 else 4)
                if first and X:
                    pe.wait_ge(norm_done, 2 * X - 1 + half)
                if n % NC in DIAG:
                    pe.wait_ge(mask_done, len(DIAG) * X + DIAG.index(n % NC) + 1)
                else:
                    pe.wait_ge(exp_done, N + 1)
                h = (Gi % NG) * HG + n // NC
                for k in range(w // P):
                    i = t0 // P + k
                    ins = mm(PS[:, 6 + half, (i % 4) * P:(i % 4 + 1) * P], pT[:, N % 4, k * P:(k + 1) * P],
                             area_v[:, (j * NH + h) * VW:(j * NH + h) * VW + P],
                             start=(first and k == 0), stop=(i == j), skip_group_check=True)
                ins.then_inc(pv_done, 1)

            def heads(Gi):
                pe.wait_ge(qc_ready, Gi + 1)
                for n in range(SLOT):
                    s_cols(Gi, n)
                    if n >= LAG:
                        pv(Gi, n - LAG)
                    if Gi + 1 < B * NG:
                        if n == AT_QK:
                            qk(Gi + 1)
                        if AT_S0 <= n < AT_MAX:
                            s_rows(Gi + 1, n - AT_S0)
                        if n == AT_MT:
                            max_rows(Gi + 1)
                    if n == AT_TR and Gi == G_LN1:
                        pe.wait_ge(qk_split, 2 * Gi + 4)
                        ln(3, 1)
                    if n == AT_CNT and Gi == G_ROUTE:
                        pe.wait_ge(qk_split, 2 * Gi + 4)
                        counts(L1)
                for n in range(SLOT - LAG, SLOT):
                    pv(Gi, n)

            def out_rows(b):
                pe.wait_ge(norm_done, 2 * NH * (b + 1))
                for i in range(HT):
                    n = HT * b + i
                    if i >= 2:
                        pe.wait_ge(yt_a, n - 1)
                        pe.wait_ge(yt_d, n - 1)
                    for c in range(8):
                        ins = nc.tensor.transpose(flat(2 * (i % 2), 2)[:, c * P:(c + 1) * P], os_[:, i, c * P:(c + 1) * P], ident)
                    ins.then_inc(yt_ps, 1)
                    if i:
                        out_proj(b, i - 1)
                out_proj(b, HT - 1)
                pe.wait_ge(wo_x, HT * (b + 1))

            def out_proj(b, i):
                n = HT * b + i
                pe.wait_ge(yt_a, n + 1)
                pe.wait_ge(yt_d, n + 1)
                if i >= 2:
                    pe.wait_ge(wo_x, n - 1)
                o = PS[:, 6 + i % 2, 0:D]
                mm(o, cst[0:1, C_ONE:C_ONE + P], brow[:], start=True, stop=False)
                for c in range(8):
                    ins = mm(o, yT[i % 2][:, c * P:(c + 1) * P], wo_in[:, c, :], start=False, stop=(c == 7))
                ins.then_inc(wo_ps, 1)

            pe.wait_ge(s_const, 16)
            pe.wait_ge(s_cst, 1)
            pe.wait_ge(s_cnn, 1)
            nc.tensor.transpose(PS[:, 6, 0:G + E], cenn[:], ident[0:G + E, 0:G + E]).then_inc(s_ct, 1)
            pe.wait_ge(s_ctc, 1)
            ln(0, 0)
            for f in range(2):
                scores(f, 0)
            for f in range(2):
                counts(f)
            pe.wait_ge(xnT_ready, 2)
            ln(1, 1)
            pe.wait_ge(sc_read, 1)
            scores(2, 1)
            pe.wait_ge(slot_ready, 1)
            counts(2)
            pe.wait_ge(s_w, N_W)
            pe.wait_ge(slot_ready, 3)
            wc2 = wcT[:].rearrange("p a d -> p (a d)")
            for c in range(8):
                mm(PS[:, 6, c * 2 * HD:(c + 1) * 2 * HD], wkT[:, c * P:(c + 1) * P], wc2, start=True, stop=True)
                mm(PS[0:2, 7, c * 2 * HD:(c + 1) * 2 * HD], bk2[:, c, :], wc2, start=True, stop=True)
            mm(PS[0:1, 7, P:2 * P], cst[0:1, C_ONE:C_ONE + 1], bor[:], start=True, stop=False)
            for c in range(8):
                ins = mm(PS[0:1, 7, P:2 * P], bvc[:, c:c + 1], wo_in[:, c, :], start=False, stop=(c == 7))
            ins.then_inc(s_wk, 1)
            pe.wait_ge(s_ax, 1)
            shared(0)
            experts(0)
            ln(2, 0)
            pe.wait_ge(xnT_ready, 6)
            for b in range(B):
                if b == 0:
                    qk(0)
                for j in range(2 if b == 0 else HT):
                    if b and j == 4:
                        pe.wait_ge(qc_ready, NG + 1)
                        ln(4, 0)
                    if b and j == 6:
                        scores(L1, 4)
                    value_tile(b, j)
                if b == 0:
                    for s in range(NS):
                        s_rows(0, s)
                        if s % 3 == 1:
                            value_half(b, 2 + s // 6, s // 3 % 2)
                    value_tile(b, 6)
                    value_tile(b, 7)
                    max_rows(0)
                pe.wait_ge(v_a, HT * (b + 1))
                pe.wait_ge(v_ones, b + 1)
                for g in range(NG):
                    heads(NG * b + g)
                out_rows(b)
            ln(5, 1)
            for f in (4, 5):
                scores(f, 5)
            for f in (4, 5):
                counts(f)
            pe.wait_ge(slot_ready, 6)
            shared(1)
            experts(1)
            for t in range(LAST_PE):
                o = PS[:, t % 4, 0:D]
                if t >= 4:
                    pe.wait_ge(last_x, t - 3)
                mm(o, ident, xs[:, HT + t, :], start=True, stop=False)
                pe.wait_ge(term, t + 1)
                for k in range(K):
                    ins = mm(o, ident, yh[:, t, k, :], start=False, stop=(k == K - 1))
                ins.then_inc(total, 1)


_INS = ['L0_attn_x', 'L0_attn_Wq', 'L0_attn_bq', 'L0_attn_Wk', 'L0_attn_bk', 'L0_attn_Wv', 'L0_attn_bv', 'L0_attn_Wo',
        'L0_attn_bo', 'L0_attn_Wc', 'L0_ffn_group_centroids', 'L0_ffn_expert_centroids', 'L0_ffn_bias', 'L0_ffn_wg',
        'L0_ffn_wu', 'L0_ffn_wd', 'L0_ffn_sg', 'L0_ffn_su', 'L0_ffn_sd']


def shape_constants():
    import numpy as np
    c = np.zeros((P, C_N), np.float32)
    p, q = np.arange(P)[:, None], np.arange(P)[None, :]
    c[:, C_ID:C_ID + P] = p == q
    c[:, C_TRI:C_TRI + P] = p <= q
    c[:, C_CS:C_CS + P] = np.where(q > p, NEG, 0.0)
    c[:, C_I8:C_I8 + G] = np.arange(G)
    c[:, C_I32:C_I32 + E] = np.arange(E)
    r = np.arange(P) % RW
    lo_q = (r >= R0 + 2 * HD) & (r < R0 + 3 * HD)
    lo_k = (r >= R0 + HD) & (r < R0 + 2 * HD)
    lo_2 = np.arange(P) == 1
    for lo, s, l in ((lo_q, C_SQ, C_LQ), (lo_k, C_SK, C_LK), (lo_2, C_S2, C_L2)):
        c[:, s] = np.where(lo, -1.0, 1.0)
        c[:, l] = lo
    c[:, C_TOK:C_TOK + NT] = LAYER - K * (q[:, 0:NT] * P + p)
    c[:, C_EID:C_EID + PT] = (q[:, 0:PT] * P + p) // CAP
    c[:, C_K:C_K + K] = np.arange(K)
    c[:, C_EPS] = 1e-5
    c[:, C_ONE:C_ONE + P] = 1.0
    return c


def layouts(inputs):
    import numpy as np
    a = {n: np.asarray(inputs[n]) for n in _INS[1:10]}
    pairs = NH * LAT // P
    return {
        'L0_attn_bq': np.stack([a['L0_attn_bq']] * 2),
        'L0_attn_Wk': a['L0_attn_Wk'].T.reshape(pairs, P, D).transpose(1, 0, 2).reshape(P, -1),
        'L0_attn_bk': np.stack([a['L0_attn_bk'].reshape(pairs, P).T] * 2, axis=2),
        'L0_attn_bv': a['L0_attn_bv'].reshape(pairs, P).T,
        'L0_attn_Wc': a['L0_attn_Wc'].T,
    }


def kernel(**inputs):
    import numpy as _np
    import concourse.bacc as _bacc
    from concourse import mybir as _mybir
    from concourse.bass_utils import run_bass_kernel_spmd as _run

    nc = _bacc.Bacc("TRN2", target_bir_lowering=False, num_devices=1)
    arrays, args = {}, []
    laid = layouts(inputs)
    for name in _INS:
        a = _np.ascontiguousarray(laid.get(name, inputs[name]))
        arrays[f"in_{name}_dram"] = a
        args.append(nc.dram_tensor(f"in_{name}_dram", a.shape, _mybir.dt.from_np(a.dtype), kind="ExternalInput").ap())
    arrays["in_consts_dram"] = shape_constants()
    args.append(nc.dram_tensor("in_consts_dram", (P, C_N), _mybir.dt.float32, kind="ExternalInput").ap())
    args.append(nc.dram_tensor("out_0_dram", (B, T, D), _mybir.dt.float32, kind="ExternalOutput").ap())
    program(nc, *args)
    r = _run(nc, [arrays], core_ids=[0])
    return r.results[0]["out_0_dram"]
```
